# Optimizing a Trainium2 kernel written in Bass

```python
import numpy as np
import jax
import jax.numpy as jnp

def _softmax(x, axis=-1):
    return jax.nn.softmax(x, axis=axis)

def _gelu(x):
    return jax.nn.gelu(x, approximate=True)

def _silu(x):
    return jax.nn.silu(x)

def _sigmoid(x):
    return jax.nn.sigmoid(x)

def _layernorm(x, axis=-1, eps=1e-05):
    m = jnp.mean(x, axis=axis, keepdims=True)
    v = jnp.var(x, axis=axis, keepdims=True)
    return (x - m) / jnp.sqrt(v + eps)

def _scatter_add(tgt, idx, src, axis=0):
    return tgt.at[idx].add(src)

def _segment_sum(src, seg, n):
    return jax.ops.segment_sum(src, seg, n)
kernel_name = 'mk_gnn_resnorm_d1_gnn_r8_6c7342'

def setup_inputs(seed: int=0):
    np.random.seed(seed)
    _w = jnp.asarray

    def _rec_inputs():
        import jax
        import jax.numpy as jnp
        _gk = jax.random.key(seed)
        x = -0.0005121 + 1.001 * jax.random.normal(jax.random.fold_in(_gk, 1), (12500, 64), jnp.float32)
        _s = jax.random.randint(jax.random.fold_in(_gk, 2), (100000,), 0, 12500, jnp.int32)
        _d = jax.random.randint(jax.random.fold_in(_gk, 3), (100000,), 0, 12500, jnp.int32)
        _loop = jnp.arange(12500, dtype=jnp.int32)
        src = jnp.concatenate([_s, _d, _loop])
        dst = jnp.concatenate([_d, _s, _loop])
        _o = jnp.argsort(dst, stable=True)
        src = src[_o]
        dst = dst[_o]
        edge_attr_32 = 0.000216709 + 1.00012 * jax.random.normal(jax.random.fold_in(_gk, 12), (212500, 32), jnp.float32)
        return (x, src, dst, edge_attr_32)
    x, src, dst, edge_attr_32 = _rec_inputs()

    def _L0_gnn_setup():
        import jax, jax.numpy as jnp
        import numpy as np
        N_NODES = 6250
        N_EDGES = 100000
        D_NODE = 64
        D_EDGE = 32
        D_HID = 128

        def _mlp(x, W1, b1, W2, b2):
            return jax.nn.relu(x @ W1 + b1) @ W2 + b2
        key = jax.random.key(seed)
        ks = jax.random.split(key, 12)
        inp = {'nodes': jax.random.normal(ks[0], (N_NODES, D_NODE), dtype=jnp.float32), 'row': jax.random.randint(ks[1], (N_EDGES,), 0, N_NODES, dtype=jnp.int32), 'col': jax.random.randint(ks[2], (N_EDGES,), 0, N_NODES, dtype=jnp.int32), 'edge_features': jax.random.normal(ks[3], (N_EDGES, D_EDGE), dtype=jnp.float32)}
        d_in_msg = 2 * D_NODE + D_EDGE
        inp['mW1'] = jax.random.normal(ks[4], (d_in_msg, D_HID), dtype=jnp.float32) / np.sqrt(d_in_msg)
        inp['mb1'] = jnp.zeros((D_HID,), dtype=jnp.float32)
        inp['mW2'] = jax.random.normal(ks[5], (D_HID, D_NODE), dtype=jnp.float32) / np.sqrt(D_HID)
        inp['mb2'] = jnp.zeros((D_NODE,), dtype=jnp.float32)
        d_in_upd = 2 * D_NODE
        inp['uW1'] = jax.random.normal(ks[6], (d_in_upd, D_HID), dtype=jnp.float32) / np.sqrt(d_in_upd)
        inp['ub1'] = jnp.zeros((D_HID,), dtype=jnp.float32)
        inp['uW2'] = jax.random.normal(ks[7], (D_HID, D_NODE), dtype=jnp.float32) / np.sqrt(D_HID)
        inp['ub2'] = jnp.zeros((D_NODE,), dtype=jnp.float32)
        return inp
    _L0_gnn_all = _L0_gnn_setup()
    _L0_gnn_in = {k: v for k, v in _L0_gnn_all.items() if k in ('mW1', 'mb1', 'mW2', 'mb2', 'uW1', 'ub1', 'uW2', 'ub2')}
    del _L0_gnn_all
    return {'x': x, 'src': src, 'dst': dst, 'edge_attr_32': edge_attr_32, 'L0_gnn_mW1': _L0_gnn_in['mW1'], 'L0_gnn_mb1': _L0_gnn_in['mb1'], 'L0_gnn_mW2': _L0_gnn_in['mW2'], 'L0_gnn_mb2': _L0_gnn_in['mb2'], 'L0_gnn_uW1': _L0_gnn_in['uW1'], 'L0_gnn_ub1': _L0_gnn_in['ub1'], 'L0_gnn_uW2': _L0_gnn_in['uW2'], 'L0_gnn_ub2': _L0_gnn_in['ub2']}

def reference(x, src, dst, edge_attr_32, L0_gnn_mW1, L0_gnn_mb1, L0_gnn_mW2, L0_gnn_mb2, L0_gnn_uW1, L0_gnn_ub1, L0_gnn_uW2, L0_gnn_ub2):
    import jax
    import jax.numpy as jnp

    def _L0_gnn_ref(nodes, row, col, edge_features, mW1, mb1, mW2, mb2, uW1, ub1, uW2, ub2):
        import jax, jax.numpy as jnp
        import numpy as np
        N_NODES = 6250
        N_EDGES = 100000
        D_NODE = 64
        D_EDGE = 32
        D_HID = 128

        def _mlp(x, W1, b1, W2, b2):
            return jax.nn.relu(x @ W1 + b1) @ W2 + b2
        msg_in = jnp.concatenate([nodes[row], nodes[col], edge_features], axis=-1)
        messages = _mlp(msg_in, mW1, mb1, mW2, mb2)
        aggregated = jax.ops.segment_sum(messages, col, num_segments=nodes.shape[0])
        upd_in = jnp.concatenate([nodes, aggregated], axis=-1)
        return _mlp(upd_in, uW1, ub1, uW2, ub2)
    x = _layernorm(x + _L0_gnn_ref(x, src, dst, edge_attr_32, L0_gnn_mW1, L0_gnn_mb1, L0_gnn_mW2, L0_gnn_mb2, L0_gnn_uW1, L0_gnn_ub1, L0_gnn_uW2, L0_gnn_ub2), axis=-1)
    return x

_drawn_inputs = setup_inputs


def setup_inputs(seed=0):
    import zlib

    import numpy as np

    out = dict(_drawn_inputs(seed))
    spreads = {'L0_gnn_mb1': (0.0, 0.1),
     'L0_gnn_mb2': (0.0, 0.1),
     'L0_gnn_ub1': (0.0, 0.437),
     'L0_gnn_ub2': (0.0, 0.358)}
    factors = {}
    for name, (base, spread) in spreads.items():
        noise = np.random.default_rng([zlib.crc32(name.encode()), seed]).standard_normal(out[name].shape)
        drawn = base * np.exp(spread * noise) if base else spread * noise
        out[name] = jnp.asarray(drawn.astype(out[name].dtype))
    for name, factor in factors.items():
        out[name] = (out[name] * factor).astype(out[name].dtype)
    return out
```

```python
from contextlib import ExitStack

import concourse.bass as bass
from concourse import mybir

F32 = mybir.dt.float32
I32 = mybir.dt.int32
ALU = mybir.AluOpType
ACT = mybir.ActivationFunctionType
AX_X = mybir.AxisListType.X

P = 128
N, E = 12500, 212500
D, DE, H = 64, 32, 128
EPS = 1e-5

TILES = 4
GE = TILES * P
NG = -(-E // GE)
TAIL = E - (NG - 1) * GE
RING = 6
ITERS = NG // RING
REST = NG - ITERS * RING
RE = E - ITERS * RING * GE
ET = -(-E // P)
WIN = P - DE
WMAX = N - WIN

NC = 192
NP = NC // 2
CHUNKS = N // NC
LAST = (N - CHUNKS * NC) // 2
LAG = 7

XC = 4 * P
XN = N // XC
XLAST = (N - XN * XC) // 4
XL = 4
TABLE = [(q, P if q < XN else XLAST) for q in range(XN + 1)]

GR = H + 1
SUM_ROWS = -(-(N + P) // P) * P

assert REST == 2 and TAIL < P and RING % 2 == 0 and 0 < LAST <= NP
assert N == 2 * (CHUNKS * NP + LAST) and N == 4 * (XN * P + XLAST) and CHUNKS > ITERS - LAG


def gnn_kernel(nc, x, xT, srcT, dst, dstT, edgeT, mW1, mb1, mW2T, mb2, uW1, ub1, uW2, ub2, out):
    table_src = nc.dram_tensor("table_src", (N, H), F32, kind="Internal").ap()
    table_dst = nc.dram_tensor("table_dst", (N, H), F32, kind="Internal").ap()
    starts_d = nc.dram_tensor("starts_d", (NG, 1), F32, kind="Internal").ap()
    sums_d = nc.dram_tensor("sums_d", (SUM_ROWS, GR), F32, kind="Internal").ap()

    with ExitStack() as ctx:
        def sb(name, shape, dt=F32):
            return ctx.enter_context(nc.sbuf_tensor(name, shape, dt))

        def pb(name, shape):
            return ctx.enter_context(nc.psum_tensor(name, shape, F32))

        def sem(name):
            return ctx.enter_context(nc.semaphore(name))

        agg = sb("agg", [P, N])
        xdeg = sb("xdeg", [P, N])
        dst_i = sb("dst_i", [P, NG * TILES], I32)
        dst_rel = sb("dst_rel", [P, NG * TILES])
        start_b = sb("start_b", [P, NG])
        start_i = sb("start_i", [1, NG], I32)
        idx = sb("idx", [P, RING, TILES], I32)
        gath = sb("gath", [P, RING, GE])
        onehot = sb("onehot", [P, RING, TILES * WIN])
        lhs = sb("lhs", [P, RING, GE])
        rhs = sb("rhs", [P, RING, H])
        hid = sb("hid", [P, RING, GE])
        deg = sb("deg", [P, RING])
        ident = sb("ident", [P, P])
        iota = sb("iota", [P, WIN])
        ones = sb("ones", [P, P])
        w_src = sb("w_src", [D, H])
        w_dst = sb("w_dst", [D, H])
        mb1b = sb("mb1b", [P, 4, H])
        mw2t = sb("mw2t", [D, H])
        mb2c = sb("mb2c", [D, D + 1])
        uw1b = sb("uw1b", [D, H])
        w_agg = sb("w_agg", [H, H])
        w_x = sb("w_x", [D + 1, H])
        ub1c = sb("ub1c", [H, 1])
        uw2 = sb("uw2", [H, D])
        ub2b = sb("ub2b", [P, 2, D])
        eps = sb("eps", [P, 1])
        upd = sb("upd", [H, NC])
        xrow = sb("xrow", [NP, 2, D])
        y = sb("y", [NP, 2, D])
        yc = sb("yc", [NP, 2, D])
        sq = sb("sq", [NP, 2, D])
        yout = sb("yout", [NP, 2, D])
        stat = sb("stat", [NP, 4, 2])
        low = sb("low", [ITERS, RING])
        high = sb("high", [ITERS, RING])
        late = sb("late", [ITERS, RING])
        bad = sb("bad", [ITERS, 1])
        bound = sb("bound", [ITERS, 1])
        dst_x = sb("dst_x", [1, RE], I32)
        low_x = sb("low_x", [1, REST])
        high_x = sb("high_x", [1, REST])
        late_x = sb("late_x", [1, REST])
        bad_x = sb("bad_x", [1, 1])
        fits = sb("fits", [1, 1], I32)

        dst_s = lhs[0:ITERS, :, :].bitcast(I32)
        rows = (gath, hid)
        g_e = lhs[WIN:P, 0, 0:P]
        g_w = rhs[WIN:P, 0, :]
        g_src = gath[:, 0, 0:H]
        g_dst = gath[:, 1, 0:H]
        g_old = gath[:, 2, 0:GR]
        g_new = gath[:, 3, 0:GR]
        g_h = hid[:, 0, 0:GR]
        g_same = lhs[:, 1, 0:P]
        g_less = lhs[:, 2, 0:P]
        g_tmp = lhs[:, 3, 0:P]
        g_col_b = lhs[:, 4, 0:P]
        g_spare, g_dcol, g_again, g_to = (deg[:, i:i + 1] for i in range(4))
        g_isrc = idx[:, 0, 0:1]
        g_idst = idx[:, 1, 0:1]
        g_iout = idx[:, 2, 0:1]

        ps_turn = [pb(f"ps_turn{i}", [P, GE]) for i in range(2)]
        ps_pre = [pb(f"ps_pre{i}", [P, GE]) for i in range(2)]
        ps_sum = [pb(f"ps_sum{i}", [P, GE]) for i in range(2)]
        ps_node = pb("ps_node", [P, GE])
        ps_iota = pb("ps_iota", [P, GE])

        weights_in = sem("weights_in")
        mb1_in = sem("mb1_in")
        node_w_in = sem("node_w_in")
        edge_w_in = sem("edge_w_in")
        dst_in = sem("dst_in")
        stats_in = sem("stats_in")
        x_in = [sem(f"x_in{i}") for i in range(-(-(XN + 1) // XL))]
        memsets = sem("memsets")
        consts = sem("consts")
        chain = sem("chain")
        rows_made = sem("rows_made")
        rows_out = [sem(f"rows_out{i}") for i in range(2)]
        rows_stored = [[sem(f"rows_stored{p}_{i}") for i in range(RING)] for p in range(2)]
        node_w = sem("node_w")
        node_w_out = sem("node_w_out")
        starts_made = sem("starts_made")
        starts_stored = sem("starts_stored")
        starts_in = sem("starts_in")
        bad_made = sem("bad_made")
        bad_summed = sem("bad_summed")
        starts_ready = sem("starts_ready")
        fits_ready = sem("fits_ready")
        iota_up = sem("iota_up")
        cleared = sem("cleared")
        idx_in = [sem(f"idx_in{i}") for i in range(RING)]
        edge_in = [sem(f"edge_in{i}") for i in range(RING)]
        win_in = [sem(f"win_in{i}") for i in range(RING)]
        gathered = [sem(f"gathered{i}") for i in range(RING)]
        onehot_made = sem("onehot_made")
        turned = sem("turned")
        lhs_made = sem("lhs_made")
        pre_made = sem("pre_made")
        hsum_made = sem("hsum_made")
        hid_made = sem("hid_made")
        summed = sem("summed")
        added = sem("added")
        xrow_in = sem("xrow_in")
        upd_pre = sem("upd_pre")
        upd_made = sem("upd_made")
        y_pre = sem("y_pre")
        y_made = sem("y_made")
        var_made = sem("var_made")
        dev_made = sem("dev_made")
        yout_made = sem("yout_made")
        out_stored = sem("out_stored")
        y_step = sem("y_step")
        inv_made = sem("inv_made")
        passed = sem("passed")
        g_consts = sem("g_consts")
        g_step = sem("g_step")
        g_isrc_in = sem("g_isrc_in")
        g_idst_in = sem("g_idst_in")
        g_e_in = sem("g_e_in")
        g_zero = sem("g_zero")
        g_cleared = sem("g_cleared")
        g_src_got = sem("g_src_got")
        g_dst_got = sem("g_dst_got")
        g_old_got = sem("g_old_got")
        g_col = sem("g_col")
        g_mm = sem("g_mm")
        g_ready = sem("g_ready")
        g_comb = sem("g_comb")
        g_done = sem("g_done")
        g_put = sem("g_put")
        g_back = sem("g_back")
        g_turn = sem("g_turn")
        g_copied = sem("g_copied")

        block = ctx.enter_context(nc.Block())

        def after(eng, s, value):
            if not isinstance(value, int) or value > 0:
                eng.wait_ge(s, value)

        def shape(group):
            return (1, TAIL) if isinstance(group, int) and group == NG else (TILES, P)

        def after(eng, s, value):
            if not isinstance(value, int) or value > 0:
                eng.wait_ge(s, value)

        def let(eng):
            eng.sem_inc(passed, 1)

        def cols(start, count):
            return slice(start, start + count) if isinstance(start, int) else bass.ds(start, count)

        def group(it, k, back=0):
            it, k = it + (k - back) // RING, (k - back) % RING
            s = it * RING + k
            return None if isinstance(s, int) and not 0 <= s < NG else (s, it, k)

        def shape(s):
            return (1, TAIL) if isinstance(s, int) and s == NG - 1 else (TILES, P)

        def groups(eng, step, node):
            for k in range(RING):
                step(0, k)
            with eng.Fori(1, LAG) as it:
                for k in range(RING):
                    step(it, k)
            with eng.Fori(LAG, ITERS) as it:
                for k in range(RING):
                    step(it, k)
                    node(it - LAG, k, NP)
            for k in range(REST + 3):
                step(ITERS, k)
            for c in range(ITERS - LAG, CHUNKS + 1):
                for k in range(RING):
                    node(c, k, NP if c < CHUNKS else LAST)

        def all_nodes(eng, node):
            for k in range(RING):
                node(0, k, NP)
            with eng.Fori(1, CHUNKS) as c:
                for k in range(RING):
                    node(c, k, NP)
            for k in range(RING):
                node(CHUNKS, k, LAST)

        def tiles(eng, tile):
            tile(0, P)
            with eng.Fori(1, ET - 1) as t:
                tile(t, P)
            tile(ET - 1, E - (ET - 1) * P)

        def blocks(eng, part):
            part(0, P)
            with eng.Fori(1, N // P) as b:
                part(b, P)
            part(N // P, N % P)

        def stored(eng, phase):
            for k in range(RING):
                eng.wait_ge(rows_stored[phase][k], 16 * sum(q % RING == k for q, _ in TABLE))

        def store_rows(eng, phase, q, m):
            eng.wait_ge(rows_out[phase], q + 1)
            to = (table_src, table_dst)[phase][q * XC:q * XC + 4 * m, :]
            eng.dma_start(to.rearrange("(p j) h -> p (j h)", j=4),
                          rows[phase][0:m, q % RING, :]).then_inc(rows_stored[phase][q % RING], 16)

        @block.sync
        def _(sp):
            def load_idx(s, it, k):
                after(sp, gathered[k], it * (16 * TILES))
                sp.dma_start(idx[:, k, :], srcT[:, cols(s * TILES, TILES)]).then_inc(idx_in[k], 16)

            sp.dma_start(w_src[:, :], mW1[0:D, :]).then_inc(weights_in, 16)
            sp.dma_start(w_dst[0:D, :], mW1[D:2 * D, :]).then_inc(weights_in, 16)

            for i in range(len(x_in)):
                at = slice(i * XL * XC, min((i + 1) * XL * XC, N))
                sp.dma_start(xdeg[0:D, at], xT[:, at]).then_inc(x_in[i], 16)
                if i == 0:
                    whole = ITERS // 16 * 16
                    by_iter = dst[0:ITERS * RING * GE].rearrange("(p r n) -> p r n", p=ITERS, r=RING)
                    sp.dma_start(dst_s[0:whole, :, :], by_iter[0:whole, :, :]).then_inc(stats_in, 16)
                    sp.dma_start(dst_s[whole:ITERS, :, :], by_iter[whole:ITERS, :, :]).then_inc(stats_in, 16)
                    sp.dma_start(dst_x[:, :], dst[E - RE:E].rearrange("(a n) -> a n", a=1)).then_inc(stats_in, 16)
            sp.dma_start(dst_i[:, :], dstT).then_inc(dst_in, 16)
            for j in range(4):
                sp.dma_start(mb1b[:, j, :], mb1.broadcast_to([P, H])).then_inc(mb1_in, 16)
            for q, m in TABLE:
                store_rows(sp, 0, q, m)
            for k in range(RING):
                sp.dma_start(rhs[WIN:P, k, :], mW1[2 * D:, :]).then_inc(edge_w_in, 16)
            sp.dma_start(mw2t[:, :], mW2T).then_inc(node_w_in, 16)
            sp.dma_start(mb2c[:, D:D + 1], mb2).then_inc(node_w_in, 16)
            sp.dma_start(uw1b[:, :], uW1[D:, :]).then_inc(node_w_in, 16)
            sp.dma_start(w_x[0:D, :], uW1[0:D, :]).then_inc(node_w_in, 16)
            sp.dma_start(ub1c[:, :], ub1).then_inc(node_w_in, 16)
            sp.dma_start(uw2[:, :], uW2).then_inc(node_w_in, 16)
            for j in range(2):
                sp.dma_start(ub2b[:, j, :], ub2.broadcast_to([P, D])).then_inc(node_w_in, 16)
            for k in range(RING):
                load_idx(k, 0, k)
            sp.wait_ge(starts_ready, 1)
            sp.wait_ge(fits_ready, 1)
            fit = sp.value_load(fits[0:1, 0:1], min_val=0, max_val=1)
            stored(sp, 1)

            def step(it, k):
                if not group(it, k):
                    return
                s, _, _ = group(it, k)
                t, m = shape(s)
                if not (isinstance(it, int) and it == 0):
                    load_idx(s, it, k)
                after(sp, pre_made, s - RING + 1)
                sp.dma_start(lhs[WIN:P, k, 0:t * m], edgeT[:, cols(s * GE, t * m)]).then_inc(edge_in[k], 16)
                start = sp.value_load(start_i[0:1, cols(s, 1)], min_val=0, max_val=WMAX)
                sp.dma_start(rhs[0:WIN, k, :], table_dst[bass.ds(start, WIN), :]).then_inc(win_in[k], 16)

            def node(c, k, m):
                at = cols(c * NC, 2 * m)
                if k == 5:
                    after(sp, y_made, c)
                    sp.dma_start(xrow[0:m, :, :], x[at, :].rearrange("(p j) f -> p j f", j=2)).then_inc(xrow_in, 16)

            with sp.If(fit == 1):
                groups(sp, step, node)
            with sp.Else():
                sp.wait_ge(g_zero, 1)
                sp.dma_start(sums_d.rearrange("(r p) g -> p r g", p=P),
                             g_new.rearrange("p (a g) -> p a g", a=1).broadcast_to([P, SUM_ROWS // P, GR])).then_inc(g_cleared, 16)

                def load(t, m):
                    if isinstance(t, int) and t == 0:
                        for k in range(RING):
                            sp.wait_ge(idx_in[k], 16)
                    after(sp, g_put, t * 16)
                    let(sp)
                    sp.dma_start(g_isrc[0:m, :], srcT[0:m, cols(t, 1)], allow_slow_non_contiguous=True).then_inc(g_isrc_in, 16)
                    sp.dma_start(g_idst[0:m, :], dstT[0:m, cols(t, 1)], allow_slow_non_contiguous=True).then_inc(g_idst_in, 16)
                    sp.dma_start(g_e[:, 0:m], edgeT[:, cols(t * P, m)]).then_inc(g_e_in, 16)

                tiles(sp, load)
                sp.wait_ge(g_put, 16 * ET)

                def back(b, m):
                    after(sp, g_turn, b)
                    sp.dma_start(g_old[0:m, :], sums_d[cols(b * P, m), :]).then_inc(g_back, 16)

                blocks(sp, back)
                all_nodes(sp, node)
            sp.wait_ge(out_stored, 16 * (CHUNKS + 1))

        @block.gpsimd
        def _(pool):
            def then(n, ins):
                ins.then_inc(consts, 1)
                pool.wait_ge(consts, n)

            then(1, nc.gpsimd.memset(ones[:, :], 1.0))
            then(2, nc.gpsimd.memset(ident[:, :], 1.0))
            then(3, nc.gpsimd.affine_select(out=ident[:, :], in_=ident[:, :], compare_op=ALU.is_equal, fill=0.0, base=0,
                                            pattern=[[-1, P]], channel_multiplier=1))
            then(4, nc.gpsimd.iota(iota[:, :], [[1, WIN]], base=0, channel_multiplier=0,
                                   allow_small_or_imprecise_dtypes=True))
            then(5, nc.gpsimd.iota(bound[:, :], [[0, 1]], base=NC * (2 - LAG), channel_multiplier=NC,
                                   allow_small_or_imprecise_dtypes=True))
            then(6, nc.gpsimd.memset(mb2c[:, 0:D], 0.0))
            then(7, nc.gpsimd.memset(eps[:, :], EPS))
            nc.gpsimd.memset(agg[:, :], 0.0).then_inc(cleared, 1)
            pool.wait_ge(cleared, 1)
            nc.gpsimd.memset(xdeg[D:D + 1, :], 0.0).then_inc(cleared, 1)
            pool.wait_ge(cleared, 2)
            pool.wait_ge(starts_made, 2)
            loop = ITERS * RING
            pool.dma_start(starts_d[0:loop, :].rearrange("(p n) a -> p (n a)", p=ITERS), low[:, :]).then_inc(starts_stored, 16)
            pool.dma_start(starts_d[loop:NG, :].rearrange("n a -> a n"), low_x[:, :]).then_inc(starts_stored, 16)
            pool.wait_ge(starts_stored, 32)
            pool.dma_start(start_b[:, :], starts_d.rearrange("n a -> a n").broadcast_to([P, NG])).then_inc(starts_in, 16)
            pool.wait_ge(fits_ready, 1)
            fit = pool.value_load(fits[0:1, 0:1], min_val=0, max_val=1)
            stored(pool, 0)

            def step(it, k):
                if not group(it, k):
                    return
                s, _, _ = group(it, k)
                t, m = shape(s)
                pool.wait_ge(idx_in[k], it * 16 + 16)
                after(pool, hsum_made, s - RING + 1)
                let(pool)
                for j in range(t):
                    pool.indirect_dma_start(gath[0:m, k, j * H:(j + 1) * H], None, table_src,
                                            bass.IndirectOffsetOnAxis(ap=idx[0:m, k, j:j + 1], axis=0)).then_inc(gathered[k], 16)

            with pool.If(fit == 1):
                groups(pool, step, lambda c, k, m: None)
            with pool.Else():
                stored(pool, 1)
                nc.gpsimd.memset(g_less, 1.0).then_inc(memsets, 1)
                pool.wait_ge(memsets, 1)
                nc.gpsimd.affine_select(out=g_less, in_=g_less, compare_op=ALU.is_gt, fill=0.0, base=0,
                                        pattern=[[-1, P]], channel_multiplier=1).then_inc(g_consts, 1)
                nc.gpsimd.iota(g_spare, [[0, 1]], base=N, channel_multiplier=1,
                               allow_small_or_imprecise_dtypes=True).then_inc(g_consts, 1)
                pool.wait_ge(g_cleared, 16)

                def tile(t, m):
                    pool.wait_ge(g_isrc_in, t * 16 + 16)
                    pool.wait_ge(g_idst_in, t * 16 + 16)
                    after(pool, g_put, t * 16)
                    let(pool)
                    for got, table, ix, done in ((g_src, table_src, g_isrc, g_src_got), (g_dst, table_dst, g_idst, g_dst_got),
                                                 (g_old, sums_d, g_idst, g_old_got)):
                        pool.indirect_dma_start(got[0:m, :], None, table,
                                                bass.IndirectOffsetOnAxis(ap=ix[0:m, :], axis=0)).then_inc(done, 16)
                    pool.wait_ge(g_done, t + 1)
                    let(pool)
                    pool.indirect_dma_start(sums_d, bass.IndirectOffsetOnAxis(ap=g_iout[0:m, :], axis=0),
                                            g_new[0:m, :], None).then_inc(g_put, 16)

                tiles(pool, tile)

        @block.tensor
        def _(pe):
            pe.wait_ge(weights_in, 32)

            def make_rows(phase):
                for q, m in TABLE:
                    pe.wait_ge(x_in[q // XL], 16)
                    if phase and q < 2:
                        pe.wait_ge(rows_out[0], len(TABLE))
                    else:
                        after(pe, rows_out[phase], q - 1)
                    for j in range(4):
                        mm = nc.tensor.matmul(ps_pre[q % 2][0:m, j * H:(j + 1) * H], xdeg[0:D, q * XC + j:q * XC + 4 * m:4],
                                              (w_src, w_dst)[phase][:, :], start=True, stop=True)
                    mm.then_inc(rows_made, 1)

            make_rows(0)
            pe.wait_ge(bad_made, 2)
            pe.wait_ge(consts, 7)
            nc.tensor.matmul(ps_turn[0][0:1, 0:1], bad[:, :], ones[0:ITERS, 0:1], start=True, stop=False)
            nc.tensor.matmul(ps_turn[0][0:1, 0:1], bad_x[:, :], ones[0:1, 0:1], start=False, stop=True).then_inc(bad_summed, 1)
            make_rows(1)
            pe.wait_ge(node_w_in, 16 * 8)
            nc.tensor.matmul(ps_node[:, 0:H], mw2t[:, :], uw1b[:, :], start=True, stop=True)
            nc.tensor.matmul(ps_node[0:D + 1, H:2 * H], mb2c[:, :], uw1b[:, :], start=True, stop=True).then_inc(node_w, 1)
            pe.wait_ge(fits_ready, 1)
            pe.wait_ge(rows_out[1], len(TABLE))
            pe.wait_ge(edge_w_in, 16 * RING)
            fit = pe.value_load(fits[0:1, 0:1], min_val=0, max_val=1)

            def turn(s, it, k):
                t, m = shape(s)
                pe.wait_ge(onehot_made, s + 1)
                after(pe, lhs_made, s - 1)
                for j in range(t):
                    mm = nc.tensor.transpose(ps_turn[k % 2][0:WIN, j * P:j * P + m],
                                             onehot[0:m, k, j * WIN:(j + 1) * WIN], ident[0:m, 0:m])
                mm.then_inc(turned, 1)

            def pre(s, it, k):
                t, m = shape(s)
                pe.wait_ge(lhs_made, s + 1)
                pe.wait_ge(edge_in[k], it * 16 + 16)
                pe.wait_ge(win_in[k], it * 16 + 16)
                after(pe, hsum_made, s - 1)
                for j in range(t):
                    mm = nc.tensor.matmul(ps_pre[k % 2][0:m, j * H:(j + 1) * H], lhs[:, k, j * P:j * P + m], rhs[:, k, :],
                                          start=True, stop=True)
                mm.then_inc(pre_made, 1)

            def summing(s, it, k):
                t, m = shape(s)
                pe.wait_ge(hid_made, s + 1)
                after(pe, added, 2 * (s - 1))
                for j in range(t):
                    nc.tensor.matmul(ps_sum[k % 2][:, 0:WIN], hid[0:m, k, j * H:(j + 1) * H],
                                     onehot[0:m, k, j * WIN:(j + 1) * WIN], start=(j == 0), stop=(j == t - 1))
                nc.tensor.matmul(ps_sum[k % 2][:, P:P + WIN], deg[0:WIN, k:k + 1].broadcast_to([WIN, P]), ident[0:WIN, 0:WIN],
                                 start=True, stop=True).then_inc(summed, 1)

            def step(it, k):
                for back, stage in ((0, turn), (1, pre), (2, summing)):
                    if group(it, k, back):
                        stage(*group(it, k, back))

            def node(c, k, m, general=False):
                if k == 0:
                    if general:
                        pe.wait_ge(g_copied, 2 * (N // P + 1))
                        after(pe, y_made, c)
                    else:
                        last = c * RING + (LAG - 1) * RING
                        pe.wait_ge(added, 2 * NG if isinstance(c, int) else 2 * last)
                        after(pe, y_made, c)
                    if isinstance(c, int) or not general:
                        pe.wait_ge(node_w_out, 2)
                    at = cols(c * NC, 2 * m)
                    nc.tensor.matmul(ps_node[:, 0:2 * m], w_agg[:, :], agg[:, at], start=True, stop=False)
                    nc.tensor.matmul(ps_node[:, 0:2 * m], w_x[:, :], xdeg[0:D + 1, at], start=False, stop=True).then_inc(upd_pre, 1)
                if k == 1:
                    pe.wait_ge(upd_made, c + 1)
                    for j in range(2):
                        mm = nc.tensor.matmul(ps_node[0:m, 2 * P + j * D:2 * P + (j + 1) * D], upd[:, j:2 * m:2], uw2[:, :],
                                              start=True, stop=True)
                    mm.then_inc(y_pre, 1)

            with pe.If(fit == 1):
                groups(pe, step, node)
            with pe.Else():
                def tile(t, m):
                    pe.wait_ge(g_e_in, t * 16 + 16)
                    pe.wait_ge(g_col, t + 1)
                    nc.tensor.matmul(ps_pre[0][0:m, 0:H], g_e[:, 0:m], g_w, start=True, stop=True)
                    nc.tensor.transpose(ps_turn[0][0:m, 0:m], g_col_b[0:m, 0:m], ident[0:m, 0:m]).then_inc(g_mm, 1)
                    pe.wait_ge(g_ready, t + 1)
                    nc.tensor.matmul(ps_sum[0][0:m, 0:GR], g_same[0:m, 0:m], g_h[0:m, :], start=True, stop=True).then_inc(g_comb, 1)

                tiles(pe, tile)

                def part(b, m):
                    pe.wait_ge(g_back, b * 16 + 16)
                    after(pe, g_copied, 2 * b)
                    nc.tensor.transpose(ps_turn[0][:, 0:m], g_old[0:m, 0:H], ident[0:m, 0:m])
                    nc.tensor.transpose(ps_turn[1][0:D + 1, 0:m], g_old[0:m, GR - D - 1:GR], ident[0:m, 0:m]).then_inc(g_turn, 1)

                blocks(pe, part)
                all_nodes(pe, lambda c, k, m: node(c, k, m, True))

        @block.scalar
        def _(act):
            for q, m in TABLE:
                act.wait_ge(rows_made, q + 1)
                after(act, rows_stored[0][q % RING], q // RING * 16)
                nc.scalar.copy(rows[0][0:m, q % RING, :], ps_pre[q % 2][0:m, :]).then_inc(rows_out[0], 1)
            for q, m in TABLE:
                store_rows(act, 1, q, m)
            act.wait_ge(node_w, 1)
            nc.scalar.copy(w_agg[:, :], ps_node[:, 0:H]).then_inc(node_w_out, 1)
            nc.scalar.copy(w_x[D:D + 1, :], ps_node[D:D + 1, H:2 * H]).then_inc(node_w_out, 1)
            act.wait_ge(fits_ready, 1)
            fit = act.value_load(fits[0:1, 0:1], min_val=0, max_val=1)

            def copy_turned(s, it, k):
                t, m = shape(s)
                act.wait_ge(turned, s + 1)
                after(act, summed, s - RING + 1)
                nc.scalar.activation(lhs[0:WIN, k, 0:t * m], ps_turn[k % 2][0:WIN, 0:t * m], ACT.Copy,
                                     accum_out=deg[0:WIN, k:k + 1]).then_inc(lhs_made, 1)

            def relu(s, it, k):
                t, m = shape(s)
                act.wait_ge(hsum_made, s + 1)
                h = hid[0:m, k, 0:t * H]
                nc.scalar.activation(h, h, ACT.Relu).then_inc(hid_made, 1)

            def step(it, k):
                for back, stage in ((0, copy_turned), (1, relu)):
                    if group(it, k, back):
                        stage(*group(it, k, back))

            def node(c, k, m):
                if k == 0:
                    act.wait_ge(upd_pre, c + 1)
                    after(act, y_pre, c)
                    nc.scalar.activation(upd[:, 0:2 * m], ps_node[:, 0:2 * m], ACT.Relu, bias=ub1c[:, 0:1]).then_inc(upd_made, 1)
                if k == 3:
                    act.wait_ge(var_made, c + 1)
                    nc.scalar.activation(stat[0:m, 3, :], stat[0:m, 2, :], ACT.Sqrt, bias=eps[0:m, 0:1], scale=1.0 / D).then_inc(dev_made, 1)
                if k == 5:
                    act.wait_ge(yout_made, c + 1)
                    act.dma_start(out[cols(c * NC, 2 * m), :].rearrange("(p j) f -> p j f", j=2),
                                  yout[0:m, :, :]).then_inc(out_stored, 16)

            with act.If(fit == 1):
                groups(act, step, node)
            with act.Else():
                def part(b, m):
                    act.wait_ge(g_turn, b + 1)
                    at = cols(b * P, m)
                    nc.scalar.copy(agg[:, at], ps_turn[0][:, 0:m]).then_inc(g_copied, 1)
                    nc.scalar.copy(xdeg[D:D + 1, at], ps_turn[1][D:D + 1, 0:m]).then_inc(g_copied, 1)

                act.wait_ge(cleared, 2)
                blocks(act, part)
                all_nodes(act, node)

        @block.vector
        def _(dve):
            steps = [0]

            def link(ins):
                steps[0] += 1
                ins.then_inc(chain, 1)
                dve.wait_ge(chain, steps[0])

            dve.wait_ge(consts, 7)
            dve.wait_ge(stats_in, 48)
            nc.vector.tensor_reduce(low[:, :], dst_s, AX_X, ALU.min)
            link(nc.vector.tensor_reduce(high[:, :], dst_s, AX_X, ALU.max))
            for g, (a, b) in enumerate(((0, GE), (GE, RE))):
                nc.vector.tensor_reduce(low_x[:, g:g + 1], dst_x[:, a:b], AX_X, ALU.min)
                link(nc.vector.tensor_reduce(high_x[:, g:g + 1], dst_x[:, a:b], AX_X, ALU.max))
            sets = ((low[:, :], high[:, :], late[:, :], bad[:, :], bound[:, 0:1]),
                    (low_x[:, :], high_x[:, :], late_x[:, :], bad_x[:, :], float(NC * (ITERS + 2 - LAG))))
            for lo, hi, la, ba, bd in sets:
                link(nc.vector.tensor_scalar(lo, lo, float(WMAX), None, ALU.min))
                link(nc.vector.tensor_tensor(hi, hi, lo, ALU.subtract))
                nc.vector.tensor_scalar(hi, hi, float(WIN - 1), 0.0, ALU.subtract, ALU.max)
                link(nc.vector.tensor_scalar(la, lo, bd, -1.0, ALU.subtract, ALU.mult))
                link(nc.vector.tensor_scalar(la, la, 0.0, None, ALU.max))
                link(nc.vector.tensor_tensor(hi, hi, la, ALU.add))
                nc.vector.tensor_reduce(ba, hi, AX_X, ALU.add).then_inc(bad_made, 1)
            dve.sem_inc(starts_made, 2)
            dve.wait_ge(starts_in, 16)
            dve.wait_ge(dst_in, 16)
            link(nc.vector.tensor_copy(dst_rel[:, :], dst_i[:, :]))
            nc.vector.tensor_copy(start_i[:, :], start_b[0:1, :])
            by_group = dst_rel[:, :].rearrange("p (s t) -> p s t", t=TILES)
            starts = start_b[:, :].rearrange("p (s a) -> p s a", a=1)
            link(nc.vector.tensor_tensor(by_group, by_group, starts.broadcast_to([P, NG, TILES]), ALU.subtract))
            link(nc.vector.tensor_copy(ps_iota[:, 0:WIN], iota[:, :]))
            dve.sem_inc(starts_ready, 1)
            dve.wait_ge(bad_summed, 1)
            nc.vector.tensor_scalar(fits[:, :], ps_turn[0][0:1, 0:1], 0.0, None, ALU.is_equal).then_inc(fits_ready, 1)

            dve.wait_ge(mb1_in, 64)
            for q, m in TABLE:
                dve.wait_ge(rows_made, len(TABLE) + q + 1)
                after(dve, rows_stored[1][q % RING], q // RING * 16)
                nc.vector.tensor_tensor(rows[1][0:m, q % RING, :].rearrange("p (j h) -> p j h", j=4),
                                        ps_pre[q % 2][0:m, :].rearrange("p (j h) -> p j h", j=4), mb1b[0:m, :, :],
                                        ALU.add).then_inc(rows_out[1], 1)
            dve.wait_ge(fits_ready, 1)
            fit = dve.value_load(fits[0:1, 0:1], min_val=0, max_val=1)

            def onehots(s, it, k):
                t, m = shape(s)
                after(dve, summed, s - RING + 1)
                to = onehot[0:m, k, 0:t * WIN].rearrange("p (t w) -> p t w", t=t)
                at = dst_rel[0:m, cols(s * TILES, t)].rearrange("p (t a) -> p t a", a=1)
                nums = ps_iota[0:m, 0:WIN].rearrange("p (a w) -> p a w", a=1)
                nc.vector.tensor_tensor(to, nums.broadcast_to([m, t, WIN]), at.broadcast_to([m, t, WIN]),
                                        ALU.is_equal).then_inc(onehot_made, 1)

            def add_gathered(s, it, k):
                t, m = shape(s)
                dve.wait_ge(pre_made, s + 1)
                dve.wait_ge(gathered[k], it * (16 * TILES) + 16 * t)
                after(dve, summed, s - RING + 1)
                nc.vector.tensor_tensor(hid[0:m, k, 0:t * H], ps_pre[k % 2][0:m, 0:t * H], gath[0:m, k, 0:t * H],
                                        ALU.add).then_inc(hsum_made, 1)

            def add_sums(s, it, k):
                dve.wait_ge(summed, s + 1)
                after(dve, added, 2 * s)
                start = dve.value_load(start_i[0:1, cols(s, 1)], min_val=0, max_val=WMAX)
                at = bass.ds(start, WIN)
                nc.vector.tensor_tensor(agg[:, at], agg[:, at], ps_sum[k % 2][:, 0:WIN], ALU.add).then_inc(added, 1)
                nc.vector.tensor_tensor(xdeg[D:D + 1, at], xdeg[D:D + 1, at], ps_sum[k % 2][D:D + 1, P:P + WIN],
                                        ALU.add).then_inc(added, 1)

            def step(it, k):
                for back, stage in ((0, onehots), (1, add_gathered), (3, add_sums)):
                    if group(it, k, back):
                        stage(*group(it, k, back))

            def node(c, k, m):
                whole = [m, 2, D]
                if k == 2:
                    dve.wait_ge(y_pre, c + 1)
                    dve.wait_ge(xrow_in, c * 16 + 16)
                    after(dve, yout_made, c)
                    nc.vector.tensor_tensor(y[0:m, :, :], ps_node[0:m, 2 * P:2 * P + 2 * D].rearrange("p (j f) -> p j f", j=2),
                                            xrow[0:m, :, :], ALU.add).then_inc(y_step, 1)
                    dve.wait_ge(y_step, c * 5 + 1)
                    nc.vector.tensor_tensor(y[0:m, :, :], y[0:m, :, :], ub2b[0:m, :, :], ALU.add).then_inc(y_step, 1)
                    dve.wait_ge(y_step, c * 5 + 2)
                    nc.vector.tensor_reduce(stat[0:m, 0, :], y[0:m, :, :], AX_X, ALU.add).then_inc(y_step, 1)
                    dve.wait_ge(y_step, c * 5 + 3)
                    nc.vector.tensor_scalar(stat[0:m, 1, :], stat[0:m, 0, :], 1.0 / D, None, ALU.mult).then_inc(y_step, 1)
                    dve.wait_ge(y_step, c * 5 + 4)
                    mean = stat[0:m, 1, :].rearrange("p (j a) -> p j a", a=1)
                    nc.vector.tensor_tensor(yc[0:m, :, :], y[0:m, :, :], mean.broadcast_to(whole), ALU.subtract).then_inc(y_step, 1)
                    dve.wait_ge(y_step, c * 5 + 5)
                    nc.vector.tensor_tensor(sq[0:m, :, :], yc[0:m, :, :], yc[0:m, :, :], ALU.mult).then_inc(y_made, 1)
                    dve.wait_ge(y_made, c + 1)
                    nc.vector.tensor_reduce(stat[0:m, 2, :], sq[0:m, :, :], AX_X, ALU.add).then_inc(var_made, 1)
                if k == 4:
                    dve.wait_ge(dev_made, c + 1)
                    after(dve, out_stored, c * 16)
                    nc.vector.reciprocal(stat[0:m, 0, :], stat[0:m, 3, :]).then_inc(inv_made, 1)
                    dve.wait_ge(inv_made, c + 1)
                    inv = stat[0:m, 0, :].rearrange("p (j a) -> p j a", a=1)
                    nc.vector.tensor_tensor(yout[0:m, :, :], yc[0:m, :, :], inv.broadcast_to(whole), ALU.mult).then_inc(yout_made, 1)

            dve.wait_ge(cleared, 2)
            dve.wait_ge(node_w_in, 16 * 8)
            with dve.If(fit == 1):
                groups(dve, step, node)
            with dve.Else():
                stored(dve, 1)
                nc.vector.memset(g_new, 0.0).then_inc(g_zero, 1)
                link(nc.vector.memset(g_h[:, H:GR], 1.0))
                dve.wait_ge(g_consts, 2)
                dve.wait_ge(g_cleared, 16)

                def tile(t, m):
                    def then(ins, n):
                        ins.then_inc(g_step, 1)
                        dve.wait_ge(g_step, t * 10 + n)

                    dve.wait_ge(g_idst_in, t * 16 + 16)
                    then(nc.vector.tensor_copy(g_dcol[0:m, :], g_idst[0:m, :]), 1)
                    nc.vector.tensor_copy(g_col_b[0:m, :], g_dcol[0:m, :].broadcast_to([m, P])).then_inc(g_col, 1)
                    dve.wait_ge(g_mm, t + 1)
                    then(nc.vector.tensor_scalar(g_same[0:m, 0:m], ps_turn[0][0:m, 0:m], g_dcol[0:m, :], None, ALU.is_equal), 2)
                    then(nc.vector.tensor_tensor(g_tmp[0:m, 0:m], g_same[0:m, 0:m], g_less[0:m, 0:m], ALU.mult), 3)
                    then(nc.vector.tensor_reduce(g_again[0:m, :], g_tmp[0:m, 0:m], AX_X, ALU.max), 4)
                    then(nc.vector.tensor_tensor(g_to[0:m, :], g_spare[0:m, :], g_dcol[0:m, :], ALU.subtract), 5)
                    then(nc.vector.tensor_tensor(g_to[0:m, :], g_to[0:m, :], g_again[0:m, :], ALU.mult), 6)
                    then(nc.vector.tensor_tensor(g_iout[0:m, :], g_to[0:m, :], g_dcol[0:m, :], ALU.add), 7)
                    for got in (g_src_got, g_dst_got, g_old_got):
                        dve.wait_ge(got, t * 16 + 16)
                    then(nc.vector.tensor_tensor(g_h[0:m, 0:H], g_src[0:m, :], g_dst[0:m, :], ALU.add), 8)
                    then(nc.vector.tensor_tensor(g_h[0:m, 0:H], g_h[0:m, 0:H], ps_pre[0][0:m, 0:H], ALU.add), 9)
                    then(nc.vector.tensor_scalar(g_h[0:m, 0:H], g_h[0:m, 0:H], 0.0, None, ALU.max), 10)
                    dve.sem_inc(g_ready, 1)
                    dve.wait_ge(g_comb, t + 1)
                    nc.vector.tensor_tensor(g_new[0:m, :], g_old[0:m, :], ps_sum[0][0:m, 0:GR], ALU.add).then_inc(g_done, 1)

                tiles(dve, tile)
                all_nodes(dve, node)


def kernel(**inputs):
    import numpy as _np
    import concourse.bacc as _bacc
    from concourse import mybir as _mybir
    from concourse.bass_utils import run_bass_kernel_spmd as _run

    given = {name: _np.asarray(a) for name, a in inputs.items()}

    def by_tile(a):
        return _np.pad(a, (0, NG * GE - E)).reshape(NG * TILES, P).T

    w = {name[len("L0_gnn_"):]: a for name, a in given.items() if name.startswith("L0_gnn_")}
    laid = [
        given["x"], given["x"].T, by_tile(given["src"]), given["dst"], by_tile(given["dst"]), given["edge_attr_32"].T,
        w["mW1"], w["mb1"].reshape(1, H), w["mW2"].T, w["mb2"].reshape(D, 1),
        w["uW1"], w["ub1"].reshape(H, 1), w["uW2"], w["ub2"].reshape(1, D),
    ]
    names = ["x", "xT", "srcT", "dst", "dstT", "edgeT", "mW1", "mb1", "mW2T", "mb2", "uW1", "ub1", "uW2", "ub2"]
    nc = _bacc.Bacc("TRN2", target_bir_lowering=False, num_devices=1)
    arrays, args = {}, []
    for name, a in zip(names, laid):
        a = _np.ascontiguousarray(a)
        arrays[f"in_{name}_dram"] = a
        args.append(nc.dram_tensor(f"in_{name}_dram", a.shape, _mybir.dt.from_np(a.dtype), kind="ExternalInput").ap())
    args.append(nc.dram_tensor("out_0_dram", (N, D), F32, kind="ExternalOutput").ap())
    gnn_kernel(nc, *args)
    r = _run(nc, [arrays], core_ids=[0])
    return r.results[0]["out_0_dram"]
```

```python
from contextlib import ExitStack

import concourse.bass as bass
from concourse import mybir

F32 = mybir.dt.float32
I32 = mybir.dt.int32
ALU = mybir.AluOpType
ACT = mybir.ActivationFunctionType
AX_X = mybir.AxisListType.X

P = 128
N, E = 12500, 212500
D, DE, H = 64, 32, 128
EPS = 1e-5

TILES = 4
GE = TILES * P
NG = -(-E // GE)
TAIL = E - (NG - 1) * GE
RING = 6
ITERS = NG // RING
REST = NG - ITERS * RING
RE = E - ITERS * RING * GE
ET = -(-E // P)
WIN = P - DE
WMAX = N - WIN

NC = 192
NP = NC // 2
CHUNKS = N // NC
LAST = (N - CHUNKS * NC) // 2
LAG = 7

ENDS = CHUNKS + 1 - (ITERS - LAG)

XC = 4 * P
XN = N // XC
XLAST = (N - XN * XC) // 4
XL = 4
TABLE = [(q, P if q < XN else XLAST) for q in range(XN + 1)]

GR = H + 1
SUM_ROWS = -(-(N + P) // P) * P

assert REST == 2 and TAIL < P and RING % 2 == 0 and 0 < LAST <= NP
assert N == 2 * (CHUNKS * NP + LAST) and N == 4 * (XN * P + XLAST) and CHUNKS > ITERS - LAG


def gnn_kernel(nc, x, xT, srcT, dst, dstT, edgeT, mW1, mb1, mW2T, mb2, uW1, ub1, uW2, ub2, out):
    table_src = nc.dram_tensor("table_src", (N, H), F32, kind="Internal").ap()
    table_dst = nc.dram_tensor("table_dst", (N, H), F32, kind="Internal").ap()
    starts_d = nc.dram_tensor("starts_d", (NG, 1), F32, kind="Internal").ap()
    sums_d = nc.dram_tensor("sums_d", (SUM_ROWS, GR), F32, kind="Internal").ap()

    with ExitStack() as ctx:
        def sb(name, shape, dt=F32):
            return ctx.enter_context(nc.sbuf_tensor(name, shape, dt))

        def pb(name, shape):
            return ctx.enter_context(nc.psum_tensor(name, shape, F32))

        def sem(name):
            return ctx.enter_context(nc.semaphore(name))

        agg = sb("agg", [P, N])
        xdeg = sb("xdeg", [P, N])
        dst_i = sb("dst_i", [P, NG * TILES], I32)
        dst_rel = sb("dst_rel", [P, NG * TILES])
        start_b = sb("start_b", [P, NG])
        start_i = sb("start_i", [1, NG], I32)
        idx = sb("idx", [P, RING, TILES], I32)
        gath = sb("gath", [P, RING, GE])
        onehot = sb("onehot", [P, RING, TILES * WIN])
        lhs = sb("lhs", [P, RING, GE])
        rhs = sb("rhs", [P, RING, H])
        xwin = sb("xwin", [D + 1, RING, WIN])
        hid = sb("hid", [P, RING, GE])
        deg = sb("deg", [P, RING])
        ident = sb("ident", [P, P])
        iota = sb("iota", [P, WIN])
        ones = sb("ones", [P, P])
        w_src = sb("w_src", [P, H])
        w_dst = sb("w_dst", [D + 1, H])
        mw2t = sb("mw2t", [D, H])
        mb2c = sb("mb2c", [D, D + 1])
        uw1b = sb("uw1b", [D, H])
        w_agg = sb("w_agg", [H, H])
        w_x = sb("w_x", [D + 1, H])
        ub1c = sb("ub1c", [H, 1])
        uw2 = sb("uw2", [H, D])
        ub2r = sb("ub2r", [1, D])
        eps = sb("eps", [P, 1])
        upd = sb("upd", [H, ENDS, NC])
        xrow = sb("xrow", [NP, ENDS, 2, D])
        y = sb("y", [NP, ENDS, 2, D])
        yc = sb("yc", [NP, ENDS, 2, D])
        sq = sb("sq", [NP, ENDS, 2, D])
        yout = sb("yout", [NP, ENDS, 2, D])
        stat = sb("stat", [NP, ENDS, 4, 2])
        low = sb("low", [ITERS, RING])
        high = sb("high", [ITERS, RING])
        late = sb("late", [ITERS, RING])
        bad = sb("bad", [ITERS, 1])
        bound = sb("bound", [ITERS, 1])
        dst_x = sb("dst_x", [1, RE], I32)
        low_x = sb("low_x", [1, REST])
        high_x = sb("high_x", [1, REST])
        late_x = sb("late_x", [1, REST])
        bad_x = sb("bad_x", [1, 1])
        fits = sb("fits", [1, 1], I32)

        dst_s = lhs[0:ITERS, :, :].bitcast(I32)
        rows = (gath, hid)
        g_e = lhs[WIN:P, 0, 0:P]
        g_w = rhs[WIN:P, 0, :]
        g_src = gath[:, 0, 0:H]
        g_dst = gath[:, 1, 0:H]
        g_old = gath[:, 2, 0:GR]
        g_new = gath[:, 3, 0:GR]
        g_h = hid[:, 0, 0:GR]
        g_same = lhs[:, 1, 0:P]
        g_less = lhs[:, 2, 0:P]
        g_tmp = lhs[:, 3, 0:P]
        g_col_b = lhs[:, 4, 0:P]
        g_spare, g_dcol, g_again, g_to = (deg[:, i:i + 1] for i in range(4))
        mb1b = onehot[:, 0, 0:H]
        g_isrc = idx[:, 0, 0:1]
        g_idst = idx[:, 1, 0:1]
        g_iout = idx[:, 2, 0:1]

        ps_turn = [pb(f"ps_turn{i}", [P, GE]) for i in range(2)]
        ps_pre = [pb(f"ps_pre{i}", [P, GE]) for i in range(2)]
        ps_sum = [pb(f"ps_sum{i}", [P, GE]) for i in range(2)]
        ps_node = pb("ps_node", [P, GE])
        ps_iota = pb("ps_iota", [P, GE])
        ps_ends = [ps_node, ps_pre[0], ps_pre[1], ps_turn[0], ps_turn[1]][0:ENDS]

        weights_in = sem("weights_in")
        mb1_in = sem("mb1_in")
        node_w_in = sem("node_w_in")
        edge_w_in = sem("edge_w_in")
        dst_in = sem("dst_in")
        stats_in = sem("stats_in")
        x_in = [sem(f"x_in{i}") for i in range(-(-(XN + 1) // XL))]
        memsets = sem("memsets")
        consts = sem("consts")
        chain = sem("chain")
        rows_made = sem("rows_made")
        rows_out = [sem(f"rows_out{i}") for i in range(2)]
        rows_stored = [[sem(f"rows_stored{p}_{i}") for i in range(RING)] for p in range(2)]
        node_w = sem("node_w")
        node_w_out = sem("node_w_out")
        starts_made = sem("starts_made")
        starts_stored = sem("starts_stored")
        starts_in = sem("starts_in")
        bad_made = sem("bad_made")
        bad_summed = sem("bad_summed")
        starts_ready = sem("starts_ready")
        fits_ready = sem("fits_ready")
        iota_up = sem("iota_up")
        cleared = sem("cleared")
        xdeg_zero = sem("xdeg_zero")
        idx_in = [sem(f"idx_in{i}") for i in range(RING)]
        edge_in = [sem(f"edge_in{i}") for i in range(RING)]
        win_in = [sem(f"win_in{i}") for i in range(RING)]
        win_made = sem("win_made")
        rhs_made = sem("rhs_made")
        gathered = [sem(f"gathered{i}") for i in range(RING)]
        onehot_made = sem("onehot_made")
        turned = sem("turned")
        lhs_made = sem("lhs_made")
        pre_made = sem("pre_made")
        hsum_made = sem("hsum_made")
        hid_made = sem("hid_made")
        summed = sem("summed")
        added = sem("added")
        xrow_in = [sem(f"xrow_in{i}") for i in range(ENDS)]
        upd_pre = sem("upd_pre")
        upd_made = sem("upd_made")
        y_pre = sem("y_pre")
        y_made = sem("y_made")
        var_made = sem("var_made")
        dev_made = sem("dev_made")
        yout_made = sem("yout_made")
        out_stored = [sem(f"out_stored{i}") for i in range(ENDS)]
        y_sum = sem("y_sum")
        yc_made = sem("yc_made")
        inv_made = sem("inv_made")
        passed = sem("passed")
        g_consts = sem("g_consts")
        g_step = sem("g_step")
        g_isrc_in = sem("g_isrc_in")
        g_idst_in = sem("g_idst_in")
        g_e_in = sem("g_e_in")
        g_zero = sem("g_zero")
        g_cleared = sem("g_cleared")
        g_src_got = sem("g_src_got")
        g_dst_got = sem("g_dst_got")
        g_old_got = sem("g_old_got")
        g_col = sem("g_col")
        g_mm = sem("g_mm")
        g_ready = sem("g_ready")
        g_comb = sem("g_comb")
        g_done = sem("g_done")
        g_put = sem("g_put")
        g_back = sem("g_back")
        g_turn = sem("g_turn")
        g_copied = sem("g_copied")

        block = ctx.enter_context(nc.Block())

        def after(eng, s, value):
            if not isinstance(value, int) or value > 0:
                eng.wait_ge(s, value)

        def shape(group):
            return (1, TAIL) if isinstance(group, int) and group == NG else (TILES, P)

        def after(eng, s, value):
            if not isinstance(value, int) or value > 0:
                eng.wait_ge(s, value)

        def let(eng):
            eng.sem_inc(passed, 1)

        def cols(start, count):
            return slice(start, start + count) if isinstance(start, int) else bass.ds(start, count)

        def group(it, k, back=0):
            it, k = it + (k - back) // RING, (k - back) % RING
            s = it * RING + k
            return None if isinstance(s, int) and not 0 <= s < NG else (s, it, k)

        def shape(s):
            return (1, TAIL) if isinstance(s, int) and s == NG - 1 else (TILES, P)

        def groups(eng, step, node):
            for k in range(RING):
                step(0, k)
            with eng.Fori(1, LAG) as it:
                for k in range(RING):
                    step(it, k)
            with eng.Fori(LAG, ITERS) as it:
                for k in range(RING):
                    step(it, k)
                    node(it - LAG, k, NP)
            for k in range(REST + 3):
                step(ITERS, k)
            for k in range(RING):
                for i in range(ENDS):
                    c = ITERS - LAG + i
                    node(c, k, NP if c < CHUNKS else LAST, i)

        def free(c, slot):
            return c - slot if isinstance(c, int) else c

        def all_nodes(eng, node):
            for k in range(RING):
                node(0, k, NP)
            with eng.Fori(1, CHUNKS) as c:
                for k in range(RING):
                    node(c, k, NP)
            for k in range(RING):
                node(CHUNKS, k, LAST)

        def tiles(eng, tile):
            tile(0, P)
            with eng.Fori(1, ET - 1) as t:
                tile(t, P)
            tile(ET - 1, E - (ET - 1) * P)

        def blocks(eng, part):
            part(0, P)
            with eng.Fori(1, N // P) as b:
                part(b, P)
            part(N // P, N % P)

        def stored(eng, phase):
            for k in range(RING):
                eng.wait_ge(rows_stored[phase][k], 16 * sum(q % RING == k for q, _ in TABLE))

        def store_rows(eng, phase, q, m):
            eng.wait_ge(rows_out[phase], q + 1)
            to = (table_src, table_dst)[phase][q * XC:q * XC + 4 * m, :]
            eng.dma_start(to.rearrange("(p j) h -> p (j h)", j=4),
                          rows[phase][0:m, q % RING, :]).then_inc(rows_stored[phase][q % RING], 16)

        @block.sync
        def _(sp):
            def load_idx(s, it, k):
                after(sp, gathered[k], it * (16 * TILES))
                sp.dma_start(idx[:, k, :], srcT[:, cols(s * TILES, TILES)]).then_inc(idx_in[k], 16)

            sp.dma_start(w_src[0:D, :], mW1[0:D, :]).then_inc(weights_in, 16)
            sp.dma_start(w_dst[0:D, :], mW1[D:2 * D, :]).then_inc(weights_in, 16)
            sp.dma_start(w_dst[D:D + 1, :], mb1).then_inc(weights_in, 16)

            for i in range(len(x_in)):
                at = slice(i * XL * XC, min((i + 1) * XL * XC, N))
                sp.dma_start(xdeg[0:D, at], xT[:, at]).then_inc(x_in[i], 16)
                if i == 0:
                    whole = ITERS // 16 * 16
                    by_iter = dst[0:ITERS * RING * GE].rearrange("(p r n) -> p r n", p=ITERS, r=RING)
                    sp.dma_start(dst_s[0:whole, :, :], by_iter[0:whole, :, :]).then_inc(stats_in, 16)
                    sp.dma_start(dst_s[whole:ITERS, :, :], by_iter[whole:ITERS, :, :]).then_inc(stats_in, 16)
                    sp.dma_start(dst_x[:, :], dst[E - RE:E].rearrange("(a n) -> a n", a=1)).then_inc(stats_in, 16)
            sp.dma_start(dst_i[:, :], dstT).then_inc(dst_in, 16)
            for q, m in TABLE:
                store_rows(sp, 0, q, m)
            for k in range(RING):
                sp.dma_start(rhs[WIN:P, k, :], mW1[2 * D:, :]).then_inc(edge_w_in, 16)
            sp.dma_start(mw2t[:, :], mW2T).then_inc(node_w_in, 16)
            sp.dma_start(mb2c[:, D:D + 1], mb2).then_inc(node_w_in, 16)
            sp.dma_start(uw1b[:, :], uW1[D:, :]).then_inc(node_w_in, 16)
            sp.dma_start(w_x[0:D, :], uW1[0:D, :]).then_inc(node_w_in, 16)
            sp.dma_start(ub1c[:, :], ub1).then_inc(node_w_in, 16)
            sp.dma_start(uw2[:, :], uW2).then_inc(node_w_in, 16)
            sp.dma_start(ub2r[:, :], ub2).then_inc(node_w_in, 16)
            for k in range(RING):
                load_idx(k, 0, k)
            sp.wait_ge(starts_ready, 1)
            sp.wait_ge(fits_ready, 1)
            fit = sp.value_load(fits[0:1, 0:1], min_val=0, max_val=1)

            def step(it, k):
                if not group(it, k):
                    return
                s, _, _ = group(it, k)
                t, m = shape(s)
                if not (isinstance(it, int) and it == 0):
                    load_idx(s, it, k)
                after(sp, pre_made, s - RING + 1)
                sp.dma_start(lhs[WIN:P, k, 0:t * m], edgeT[:, cols(s * GE, t * m)]).then_inc(edge_in[k], 16)
                start = sp.value_load(start_i[0:1, cols(s, 1)], min_val=0, max_val=WMAX)
                sp.dma_start(xwin[0:D, k, :], xT[:, bass.ds(start, WIN)]).then_inc(win_in[k], 16)

            def node(c, k, m, i=0):
                if k == 5:
                    after(sp, y_made, free(c, i))
                    sp.dma_start(xrow[0:m, i, :, :], x[cols(c * NC, 2 * m), :].rearrange("(p j) f -> p j f", j=2)).then_inc(xrow_in[i], 16)

            with sp.If(fit == 1):
                groups(sp, step, node)
                for i in range(ENDS):
                    sp.wait_ge(out_stored[i], 16 if i else 16 * (ITERS - LAG + 1))
            with sp.Else():
                sp.dma_start(mb1b, mb1.broadcast_to([P, H])).then_inc(mb1_in, 16)
                sp.wait_ge(g_zero, 1)
                sp.dma_start(sums_d.rearrange("(r p) g -> p r g", p=P),
                             g_new.rearrange("p (a g) -> p a g", a=1).broadcast_to([P, SUM_ROWS // P, GR])).then_inc(g_cleared, 16)

                def load(t, m):
                    if isinstance(t, int) and t == 0:
                        for k in range(RING):
                            sp.wait_ge(idx_in[k], 16)
                    after(sp, g_put, t * 16)
                    let(sp)
                    sp.dma_start(g_isrc[0:m, :], srcT[0:m, cols(t, 1)], allow_slow_non_contiguous=True).then_inc(g_isrc_in, 16)
                    sp.dma_start(g_idst[0:m, :], dstT[0:m, cols(t, 1)], allow_slow_non_contiguous=True).then_inc(g_idst_in, 16)
                    sp.dma_start(g_e[:, 0:m], edgeT[:, cols(t * P, m)]).then_inc(g_e_in, 16)

                tiles(sp, load)
                sp.wait_ge(g_put, 16 * ET)

                def back(b, m):
                    after(sp, g_turn, b)
                    sp.dma_start(g_old[0:m, :], sums_d[cols(b * P, m), :]).then_inc(g_back, 16)

                blocks(sp, back)
                all_nodes(sp, node)
                sp.wait_ge(out_stored[0], 16 * (CHUNKS + 1))

        @block.gpsimd
        def _(pool):
            def then(n, ins):
                ins.then_inc(consts, 1)
                pool.wait_ge(consts, n)

            then(1, nc.gpsimd.memset(ones[:, :], 1.0))
            then(2, nc.gpsimd.memset(ident[:, :], 1.0))
            then(3, nc.gpsimd.affine_select(out=ident[:, :], in_=ident[:, :], compare_op=ALU.is_equal, fill=0.0, base=0,
                                            pattern=[[-1, P]], channel_multiplier=1))
            then(4, nc.gpsimd.iota(iota[:, :], [[1, WIN]], base=0, channel_multiplier=0,
                                   allow_small_or_imprecise_dtypes=True))
            then(5, nc.gpsimd.iota(bound[:, :], [[0, 1]], base=NC * (2 - LAG), channel_multiplier=NC,
                                   allow_small_or_imprecise_dtypes=True))
            then(6, nc.gpsimd.memset(mb2c[:, 0:D], 0.0))
            then(7, nc.gpsimd.memset(eps[:, :], EPS))
            then(8, nc.gpsimd.memset(xwin[D:D + 1, :, :], 1.0))
            nc.gpsimd.memset(agg[:, :], 0.0).then_inc(cleared, 1)
            pool.wait_ge(cleared, 1)
            pool.wait_ge(starts_made, 2)
            loop = ITERS * RING
            pool.dma_start(starts_d[0:loop, :].rearrange("(p n) a -> p (n a)", p=ITERS), low[:, :]).then_inc(starts_stored, 16)
            pool.dma_start(starts_d[loop:NG, :].rearrange("n a -> a n"), low_x[:, :]).then_inc(starts_stored, 16)
            pool.wait_ge(starts_stored, 32)
            pool.dma_start(start_b[:, :], starts_d.rearrange("n a -> a n").broadcast_to([P, NG])).then_inc(starts_in, 16)
            pool.wait_ge(fits_ready, 1)
            fit = pool.value_load(fits[0:1, 0:1], min_val=0, max_val=1)
            stored(pool, 0)

            def step(it, k):
                if not group(it, k):
                    return
                s, _, _ = group(it, k)
                t, m = shape(s)
                pool.wait_ge(idx_in[k], it * 16 + 16)
                after(pool, hsum_made, s - RING + 1)
                let(pool)
                for j in range(t):
                    pool.indirect_dma_start(gath[0:m, k, j * H:(j + 1) * H], None, table_src,
                                            bass.IndirectOffsetOnAxis(ap=idx[0:m, k, j:j + 1], axis=0)).then_inc(gathered[k], 16)

            with pool.If(fit == 1):
                groups(pool, step, lambda *chunk: None)
            with pool.Else():
                stored(pool, 1)
                nc.gpsimd.memset(g_less, 1.0).then_inc(memsets, 1)
                pool.wait_ge(memsets, 1)
                nc.gpsimd.affine_select(out=g_less, in_=g_less, compare_op=ALU.is_gt, fill=0.0, base=0,
                                        pattern=[[-1, P]], channel_multiplier=1).then_inc(g_consts, 1)
                nc.gpsimd.iota(g_spare, [[0, 1]], base=N, channel_multiplier=1,
                               allow_small_or_imprecise_dtypes=True).then_inc(g_consts, 1)
                pool.wait_ge(g_cleared, 16)

                def tile(t, m):
                    pool.wait_ge(g_isrc_in, t * 16 + 16)
                    pool.wait_ge(g_idst_in, t * 16 + 16)
                    after(pool, g_put, t * 16)
                    let(pool)
                    for got, table, ix, done in ((g_src, table_src, g_isrc, g_src_got), (g_dst, table_dst, g_idst, g_dst_got),
                                                 (g_old, sums_d, g_idst, g_old_got)):
                        pool.indirect_dma_start(got[0:m, :], None, table,
                                                bass.IndirectOffsetOnAxis(ap=ix[0:m, :], axis=0)).then_inc(done, 16)
                    pool.wait_ge(g_done, t + 1)
                    let(pool)
                    pool.indirect_dma_start(sums_d, bass.IndirectOffsetOnAxis(ap=g_iout[0:m, :], axis=0),
                                            g_new[0:m, :], None).then_inc(g_put, 16)

                tiles(pool, tile)

        @block.tensor
        def _(pe):
            pe.wait_ge(weights_in, 48)

            def make_rows(phase):
                kk, w = ((P, w_src), (D, w_dst))[phase]
                for q, m in TABLE:
                    pe.wait_ge(x_in[q // XL], 16)
                    pe.wait_ge(xdeg_zero, q // XL + 2)
                    after(pe, rows_out[phase], q - 1)
                    for j in range(4):
                        mm = nc.tensor.matmul(ps_pre[q % 2][0:m, j * H:(j + 1) * H], xdeg[0:kk, q * XC + j:q * XC + 4 * m:4],
                                              w[0:kk, :], start=True, stop=True)
                    mm.then_inc(rows_made, 1)
                    if phase == 0 and q == 16:
                        pe.wait_ge(bad_made, 2)
                        pe.wait_ge(consts, 8)
                        nc.tensor.matmul(ps_sum[0][0:1, 0:1], bad[:, :], ones[0:ITERS, 0:1], start=True, stop=False)
                        nc.tensor.matmul(ps_sum[0][0:1, 0:1], bad_x[:, :], ones[0:1, 0:1], start=False,
                                         stop=True).then_inc(bad_summed, 1)

            make_rows(0)
            pe.wait_ge(node_w_in, 16 * 7)
            nc.tensor.matmul(ps_node[:, 0:H], mw2t[:, :], uw1b[:, :], start=True, stop=True)
            nc.tensor.matmul(ps_node[0:D + 1, H:2 * H], mb2c[:, :], uw1b[:, :], start=True, stop=True).then_inc(node_w, 1)
            pe.wait_ge(fits_ready, 1)
            pe.wait_ge(rows_out[0], len(TABLE))
            pe.wait_ge(edge_w_in, 16 * RING)
            fit = pe.value_load(fits[0:1, 0:1], min_val=0, max_val=1)

            def window(s, it, k):
                pe.wait_ge(win_in[k], it * 16 + 16)
                after(pe, added, 2 * (s - 3))
                nc.tensor.matmul(ps_sum[k % 2][0:WIN, 2 * P:3 * P], xwin[:, k, :], w_dst[:, :],
                                 start=True, stop=True).then_inc(win_made, 1)

            def turn(s, it, k):
                t, m = shape(s)
                pe.wait_ge(onehot_made, s + 1)
                after(pe, lhs_made, s - 1)
                for j in range(t):
                    mm = nc.tensor.transpose(ps_turn[k % 2][0:WIN, j * P:j * P + m],
                                             onehot[0:m, k, j * WIN:(j + 1) * WIN], ident[0:m, 0:m])
                mm.then_inc(turned, 1)

            def pre(s, it, k):
                t, m = shape(s)
                pe.wait_ge(lhs_made, s + 1)
                pe.wait_ge(edge_in[k], it * 16 + 16)
                pe.wait_ge(rhs_made, s + 1)
                after(pe, hsum_made, s - 1)
                for j in range(t):
                    mm = nc.tensor.matmul(ps_pre[k % 2][0:m, j * H:(j + 1) * H], lhs[:, k, j * P:j * P + m], rhs[:, k, :],
                                          start=True, stop=True)
                mm.then_inc(pre_made, 1)

            def summing(s, it, k):
                t, m = shape(s)
                pe.wait_ge(hid_made, s + 1)
                after(pe, added, 2 * (s - 1))
                pe.wait_ge(rhs_made, s + 3 if not isinstance(s, int) else min(s + 3, NG))
                for j in range(t):
                    nc.tensor.matmul(ps_sum[k % 2][:, 0:WIN], hid[0:m, k, j * H:(j + 1) * H],
                                     onehot[0:m, k, j * WIN:(j + 1) * WIN], start=(j == 0), stop=(j == t - 1))
                nc.tensor.matmul(ps_sum[k % 2][:, P:P + WIN], deg[0:WIN, k:k + 1].broadcast_to([WIN, P]), ident[0:WIN, 0:WIN],
                                 start=True, stop=True).then_inc(summed, 1)

            def step(it, k):
                for back, stage in ((0, turn), (1, pre), (2, summing), (-1, window)):
                    if group(it, k, back):
                        stage(*group(it, k, back))

            def node(c, k, m, i=0, general=False):
                bank = ps_ends[i]
                if k == 0:
                    if general:
                        pe.wait_ge(g_copied, 2 * (N // P + 1))
                    else:
                        last = c * RING + (LAG - 1) * RING
                        pe.wait_ge(added, 2 * NG if isinstance(c, int) else 2 * last)
                    after(pe, y_made, free(c, i))
                    if isinstance(c, int) or not general:
                        pe.wait_ge(node_w_out, 2)
                    at = cols(c * NC, 2 * m)
                    nc.tensor.matmul(bank[:, 0:2 * m], w_agg[:, :], agg[:, at], start=True, stop=False)
                    nc.tensor.matmul(bank[:, 0:2 * m], w_x[:, :], xdeg[0:D + 1, at], start=False, stop=True).then_inc(upd_pre, 1)
                if k == 1:
                    pe.wait_ge(upd_made, c + 1)
                    for j in range(2):
                        to = bank[0:m, 2 * P + j * D:2 * P + (j + 1) * D]
                        nc.tensor.matmul(to, upd[:, i, j:2 * m:2], uw2[:, :], start=True, stop=False)
                        mm = nc.tensor.matmul(to, ones[0:1, 0:m], ub2r[:, 0:D], start=False, stop=True)
                    mm.then_inc(y_pre, 1)

            with pe.If(fit == 1):
                window(0, 0, 0)
                groups(pe, step, node)
            with pe.Else():
                make_rows(1)

                def tile(t, m):
                    pe.wait_ge(g_e_in, t * 16 + 16)
                    pe.wait_ge(g_col, t + 1)
                    nc.tensor.matmul(ps_pre[0][0:m, 0:H], g_e[:, 0:m], g_w, start=True, stop=True)
                    nc.tensor.transpose(ps_turn[0][0:m, 0:m], g_col_b[0:m, 0:m], ident[0:m, 0:m]).then_inc(g_mm, 1)
                    pe.wait_ge(g_ready, t + 1)
                    nc.tensor.matmul(ps_sum[0][0:m, 0:GR], g_same[0:m, 0:m], g_h[0:m, :], start=True, stop=True).then_inc(g_comb, 1)

                tiles(pe, tile)

                def part(b, m):
                    pe.wait_ge(g_back, b * 16 + 16)
                    after(pe, g_copied, 2 * b)
                    nc.tensor.transpose(ps_turn[0][:, 0:m], g_old[0:m, 0:H], ident[0:m, 0:m])
                    nc.tensor.transpose(ps_turn[1][0:D + 1, 0:m], g_old[0:m, GR - D - 1:GR], ident[0:m, 0:m]).then_inc(g_turn, 1)

                blocks(pe, part)
                all_nodes(pe, lambda c, k, m: node(c, k, m, 0, True))

        @block.scalar
        def _(act):
            for q, m in TABLE:
                act.wait_ge(rows_made, q + 1)
                after(act, rows_stored[0][q % RING], q // RING * 16)
                nc.scalar.copy(rows[0][0:m, q % RING, :], ps_pre[q % 2][0:m, :]).then_inc(rows_out[0], 1)
            act.wait_ge(node_w, 1)
            nc.scalar.copy(w_agg[:, :], ps_node[:, 0:H]).then_inc(node_w_out, 1)
            nc.scalar.copy(w_x[D:D + 1, :], ps_node[D:D + 1, H:2 * H]).then_inc(node_w_out, 1)
            act.wait_ge(fits_ready, 1)
            fit = act.value_load(fits[0:1, 0:1], min_val=0, max_val=1)

            def copy_turned(s, it, k):
                t, m = shape(s)
                act.wait_ge(turned, s + 1)
                after(act, summed, s - RING + 1)
                nc.scalar.activation(lhs[0:WIN, k, 0:t * m], ps_turn[k % 2][0:WIN, 0:t * m], ACT.Copy,
                                     accum_out=deg[0:WIN, k:k + 1]).then_inc(lhs_made, 1)

            def relu(s, it, k):
                t, m = shape(s)
                act.wait_ge(hsum_made, s + 1)
                h = hid[0:m, k, 0:t * H]
                nc.scalar.activation(h, h, ACT.Relu).then_inc(hid_made, 1)

            def copy_window(s, it, k):
                act.wait_ge(win_made, s + 1)
                after(act, pre_made, s - RING + 1)
                nc.scalar.copy(rhs[0:WIN, k, :], ps_sum[k % 2][0:WIN, 2 * P:3 * P]).then_inc(rhs_made, 1)

            def step(it, k):
                for back, stage in ((0, copy_turned), (1, relu), (-1, copy_window)):
                    if group(it, k, back):
                        stage(*group(it, k, back))

            def node(c, k, m, i=0):
                if k == 0:
                    act.wait_ge(upd_pre, c + 1)
                    after(act, y_pre, free(c, i))
                    nc.scalar.activation(upd[:, i, 0:2 * m], ps_ends[i][:, 0:2 * m], ACT.Relu, bias=ub1c[:, 0:1]).then_inc(upd_made, 1)
                if k == 3:
                    act.wait_ge(yc_made, c + 1)
                    after(act, yout_made, free(c, i))
                    for j in range(2):
                        nc.scalar.activation(sq[0:m, i, j, :], yc[0:m, i, j, :], ACT.Square,
                                             accum_out=stat[0:m, i, 2, j:j + 1]).then_inc(var_made, 1)
                    act.wait_ge(var_made, 2 * c + 2)
                    nc.scalar.activation(stat[0:m, i, 3, :], stat[0:m, i, 2, :], ACT.Sqrt, bias=eps[0:m, 0:1],
                                         scale=1.0 / D).then_inc(dev_made, 1)
                if k == 5:
                    act.wait_ge(yout_made, c + 1)
                    act.dma_start(out[cols(c * NC, 2 * m), :].rearrange("(p j) f -> p j f", j=2),
                                  yout[0:m, i, :, :]).then_inc(out_stored[i], 16)

            with act.If(fit == 1):
                copy_window(0, 0, 0)
                groups(act, step, node)
            with act.Else():
                for q, m in TABLE:
                    store_rows(act, 1, q, m)

                def part(b, m):
                    act.wait_ge(g_turn, b + 1)
                    at = cols(b * P, m)
                    nc.scalar.copy(agg[:, at], ps_turn[0][:, 0:m]).then_inc(g_copied, 1)
                    nc.scalar.copy(xdeg[D:D + 1, at], ps_turn[1][D:D + 1, 0:m]).then_inc(g_copied, 1)

                act.wait_ge(cleared, 1)
                blocks(act, part)
                all_nodes(act, node)

        @block.vector
        def _(dve):
            steps = [0]

            def link(ins):
                steps[0] += 1
                ins.then_inc(chain, 1)
                dve.wait_ge(chain, steps[0])

            for i in range(len(x_in)):
                nc.vector.memset(xdeg[D:P, i * XL * XC:min((i + 1) * XL * XC, N)], 0.0).then_inc(xdeg_zero, 1)
                if i == 0:
                    nc.vector.memset(w_src[D:P, :], 0.0).then_inc(xdeg_zero, 1)
            dve.wait_ge(consts, 8)
            dve.wait_ge(stats_in, 48)
            nc.vector.tensor_reduce(low[:, :], dst_s, AX_X, ALU.min)
            link(nc.vector.tensor_reduce(high[:, :], dst_s, AX_X, ALU.max))
            for g, (a, b) in enumerate(((0, GE), (GE, RE))):
                nc.vector.tensor_reduce(low_x[:, g:g + 1], dst_x[:, a:b], AX_X, ALU.min)
                link(nc.vector.tensor_reduce(high_x[:, g:g + 1], dst_x[:, a:b], AX_X, ALU.max))
            sets = ((low[:, :], high[:, :], late[:, :], bad[:, :], bound[:, 0:1]),
                    (low_x[:, :], high_x[:, :], late_x[:, :], bad_x[:, :], float(NC * (ITERS + 2 - LAG))))
            for lo, hi, la, ba, bd in sets:
                link(nc.vector.tensor_scalar(lo, lo, float(WMAX), None, ALU.min))
                link(nc.vector.tensor_tensor(hi, hi, lo, ALU.subtract))
                nc.vector.tensor_scalar(hi, hi, float(WIN - 1), 0.0, ALU.subtract, ALU.max)
                link(nc.vector.tensor_scalar(la, lo, bd, -1.0, ALU.subtract, ALU.mult))
                link(nc.vector.tensor_scalar(la, la, 0.0, None, ALU.max))
                link(nc.vector.tensor_tensor(hi, hi, la, ALU.add))
                nc.vector.tensor_reduce(ba, hi, AX_X, ALU.add).then_inc(bad_made, 1)
            dve.sem_inc(starts_made, 2)
            dve.wait_ge(bad_summed, 1)
            nc.vector.tensor_scalar(fits[:, :], ps_sum[0][0:1, 0:1], 0.0, None, ALU.is_equal).then_inc(fits_ready, 1)
            dve.wait_ge(starts_in, 16)
            dve.wait_ge(dst_in, 16)
            link(nc.vector.tensor_copy(dst_rel[:, :], dst_i[:, :]))
            nc.vector.tensor_copy(start_i[:, :], start_b[0:1, :])
            by_group = dst_rel[:, :].rearrange("p (s t) -> p s t", t=TILES)
            starts = start_b[:, :].rearrange("p (s a) -> p s a", a=1)
            link(nc.vector.tensor_tensor(by_group, by_group, starts.broadcast_to([P, NG, TILES]), ALU.subtract))
            link(nc.vector.tensor_copy(ps_iota[:, 0:WIN], iota[:, :]))
            dve.sem_inc(starts_ready, 1)

            dve.wait_ge(fits_ready, 1)
            fit = dve.value_load(fits[0:1, 0:1], min_val=0, max_val=1)

            def onehots(s, it, k):
                t, m = shape(s)
                after(dve, summed, s - RING + 1)
                to = onehot[0:m, k, 0:t * WIN].rearrange("p (t w) -> p t w", t=t)
                at = dst_rel[0:m, cols(s * TILES, t)].rearrange("p (t a) -> p t a", a=1)
                nums = ps_iota[0:m, 0:WIN].rearrange("p (a w) -> p a w", a=1)
                nc.vector.tensor_tensor(to, nums.broadcast_to([m, t, WIN]), at.broadcast_to([m, t, WIN]),
                                        ALU.is_equal).then_inc(onehot_made, 1)

            def add_gathered(s, it, k):
                t, m = shape(s)
                dve.wait_ge(pre_made, s + 1)
                dve.wait_ge(gathered[k], it * (16 * TILES) + 16 * t)
                after(dve, summed, s - RING + 1)
                nc.vector.tensor_tensor(hid[0:m, k, 0:t * H], ps_pre[k % 2][0:m, 0:t * H], gath[0:m, k, 0:t * H],
                                        ALU.add).then_inc(hsum_made, 1)

            def add_sums(s, it, k):
                dve.wait_ge(summed, s + 1)
                after(dve, added, 2 * s)
                start = dve.value_load(start_i[0:1, cols(s, 1)], min_val=0, max_val=WMAX)
                at = bass.ds(start, WIN)
                nc.vector.tensor_tensor(agg[:, at], agg[:, at], ps_sum[k % 2][:, 0:WIN], ALU.add).then_inc(added, 1)
                nc.vector.tensor_tensor(xdeg[D:D + 1, at], xdeg[D:D + 1, at], ps_sum[k % 2][D:D + 1, P:P + WIN],
                                        ALU.add).then_inc(added, 1)

            def step(it, k):
                for back, stage in ((1, add_gathered), (-1, onehots), (3, add_sums)):
                    if group(it, k, back):
                        stage(*group(it, k, back))

            def node(c, k, m, i=0):
                whole = [m, 2, D]
                if k == 2:
                    dve.wait_ge(y_pre, c + 1)
                    dve.wait_ge(xrow_in[i], 16 if i else c * 16 + 16)
                    after(dve, yout_made, free(c, i))
                    nc.vector.tensor_tensor(y[0:m, i, :, :], ps_ends[i][0:m, 2 * P:2 * P + 2 * D].rearrange("p (j f) -> p j f", j=2),
                                            xrow[0:m, i, :, :], ALU.add).then_inc(y_made, 1)
                    dve.wait_ge(y_made, c + 1)
                    nc.vector.tensor_reduce(stat[0:m, i, 1, :], y[0:m, i, :, :], AX_X, ALU.add).then_inc(y_sum, 1)
                    dve.wait_ge(y_sum, c + 1)
                    total = stat[0:m, i, 1, :].rearrange("p (j a) -> p j a", a=1)
                    nc.vector.scalar_tensor_tensor(out=yc[0:m, i, :, :], in0=total.broadcast_to(whole), scalar=-1.0 / D,
                                                   in1=y[0:m, i, :, :], op0=ALU.mult, op1=ALU.add).then_inc(yc_made, 1)
                if k == 4:
                    dve.wait_ge(dev_made, c + 1)
                    after(dve, out_stored[i], 0 if i else c * 16)
                    nc.vector.reciprocal(stat[0:m, i, 0, :], stat[0:m, i, 3, :]).then_inc(inv_made, 1)
                    dve.wait_ge(inv_made, c + 1)
                    inv = stat[0:m, i, 0, :].rearrange("p (j a) -> p j a", a=1)
                    nc.vector.tensor_tensor(yout[0:m, i, :, :], yc[0:m, i, :, :], inv.broadcast_to(whole), ALU.mult).then_inc(yout_made, 1)

            dve.wait_ge(cleared, 1)
            dve.wait_ge(node_w_in, 16 * 7)
            with dve.If(fit == 1):
                onehots(0, 0, 0)
                groups(dve, step, node)
            with dve.Else():
                dve.wait_ge(mb1_in, 16)
                for q, m in TABLE:
                    dve.wait_ge(rows_made, len(TABLE) + q + 1)
                    after(dve, rows_stored[1][q % RING], q // RING * 16)
                    nc.vector.tensor_tensor(rows[1][0:m, q % RING, :].rearrange("p (j h) -> p j h", j=4),
                                            ps_pre[q % 2][0:m, :].rearrange("p (j h) -> p j h", j=4),
                                            mb1b[0:m, :].rearrange("p (a h) -> p a h", a=1).broadcast_to([m, 4, H]),
                                            ALU.add).then_inc(rows_out[1], 1)
                stored(dve, 1)
                nc.vector.memset(g_new, 0.0).then_inc(g_zero, 1)
                link(nc.vector.memset(g_h[:, H:GR], 1.0))
                dve.wait_ge(g_consts, 2)
                dve.wait_ge(g_cleared, 16)

                def tile(t, m):
                    def then(ins, n):
                        ins.then_inc(g_step, 1)
                        dve.wait_ge(g_step, t * 10 + n)

                    dve.wait_ge(g_idst_in, t * 16 + 16)
                    then(nc.vector.tensor_copy(g_dcol[0:m, :], g_idst[0:m, :]), 1)
                    nc.vector.tensor_copy(g_col_b[0:m, :], g_dcol[0:m, :].broadcast_to([m, P])).then_inc(g_col, 1)
                    dve.wait_ge(g_mm, t + 1)
                    then(nc.vector.tensor_scalar(g_same[0:m, 0:m], ps_turn[0][0:m, 0:m], g_dcol[0:m, :], None, ALU.is_equal), 2)
                    then(nc.vector.tensor_tensor(g_tmp[0:m, 0:m], g_same[0:m, 0:m], g_less[0:m, 0:m], ALU.mult), 3)
                    then(nc.vector.tensor_reduce(g_again[0:m, :], g_tmp[0:m, 0:m], AX_X, ALU.max), 4)
                    then(nc.vector.tensor_tensor(g_to[0:m, :], g_spare[0:m, :], g_dcol[0:m, :], ALU.subtract), 5)
                    then(nc.vector.tensor_tensor(g_to[0:m, :], g_to[0:m, :], g_again[0:m, :], ALU.mult), 6)
                    then(nc.vector.tensor_tensor(g_iout[0:m, :], g_to[0:m, :], g_dcol[0:m, :], ALU.add), 7)
                    for got in (g_src_got, g_dst_got, g_old_got):
                        dve.wait_ge(got, t * 16 + 16)
                    then(nc.vector.tensor_tensor(g_h[0:m, 0:H], g_src[0:m, :], g_dst[0:m, :], ALU.add), 8)
                    then(nc.vector.tensor_tensor(g_h[0:m, 0:H], g_h[0:m, 0:H], ps_pre[0][0:m, 0:H], ALU.add), 9)
                    then(nc.vector.tensor_scalar(g_h[0:m, 0:H], g_h[0:m, 0:H], 0.0, None, ALU.max), 10)
                    dve.sem_inc(g_ready, 1)
                    dve.wait_ge(g_comb, t + 1)
                    nc.vector.tensor_tensor(g_new[0:m, :], g_old[0:m, :], ps_sum[0][0:m, 0:GR], ALU.add).then_inc(g_done, 1)

                tiles(dve, tile)
                all_nodes(dve, node)


def kernel(**inputs):
    import numpy as _np
    import concourse.bacc as _bacc
    from concourse import mybir as _mybir
    from concourse.bass_utils import run_bass_kernel_spmd as _run

    given = {name: _np.asarray(a) for name, a in inputs.items()}

    def by_tile(a):
        return _np.pad(a, (0, NG * GE - E)).reshape(NG * TILES, P).T

    w = {name[len("L0_gnn_"):]: a for name, a in given.items() if name.startswith("L0_gnn_")}
    laid = [
        given["x"], given["x"].T, by_tile(given["src"]), given["dst"], by_tile(given["dst"]), given["edge_attr_32"].T,
        w["mW1"], w["mb1"].reshape(1, H), w["mW2"].T, w["mb2"].reshape(D, 1),
        w["uW1"], w["ub1"].reshape(H, 1), w["uW2"], w["ub2"].reshape(1, D),
    ]
    names = ["x", "xT", "srcT", "dst", "dstT", "edgeT", "mW1", "mb1", "mW2T", "mb2", "uW1", "ub1", "uW2", "ub2"]
    nc = _bacc.Bacc("TRN2", target_bir_lowering=False, num_devices=1)
    arrays, args = {}, []
    for name, a in zip(names, laid):
        a = _np.ascontiguousarray(a)
        arrays[f"in_{name}_dram"] = a
        args.append(nc.dram_tensor(f"in_{name}_dram", a.shape, _mybir.dt.from_np(a.dtype), kind="ExternalInput").ap())
    args.append(nc.dram_tensor("out_0_dram", (N, D), F32, kind="ExternalOutput").ap())
    gnn_kernel(nc, *args)
    r = _run(nc, [arrays], core_ids=[0])
    return r.results[0]["out_0_dram"]
```

```python
from contextlib import ExitStack

import concourse.bass as bass
from concourse import mybir

F32 = mybir.dt.float32
I32 = mybir.dt.int32
ALU = mybir.AluOpType
ACT = mybir.ActivationFunctionType
AX_X = mybir.AxisListType.X

P = 128
N, E = 12500, 212500
D, DE, H = 64, 32, 128
EPS = 1e-5

TILES = 4
GE = TILES * P
NG = -(-E // GE)
TAIL = E - (NG - 1) * GE
RING = 6
ITERS = NG // RING
REST = NG - ITERS * RING
RE = E - ITERS * RING * GE
ET = -(-E // P)
WIN = P - DE
WMAX = N - WIN

NC = 192
NP = NC // 2
CHUNKS = N // NC - 1
LAST = (N - CHUNKS * NC) // 2
LAG = 7

ENDS = CHUNKS + 1 - (ITERS - LAG)

XC = 4 * P
XN = N // XC
XLAST = (N - XN * XC) // 4
XL = 4
TABLE = [(q, P if q < XN else XLAST) for q in range(XN + 1)]

RAW = 8
FIRST = 2 * RING
LOOK = 2
DFIRST = 8 * RING
ZEROS_ACT = (1, 3)
ZEROS_DVE = (0, 2, 4, 5, 6)
Q_FITS = 13
Q_WEIGHTS = 18
Q_LOADS = 17
EARLY = {23: 0, 24: 1}
Q_DST = 8

AHEAD, UPD, Y, CENTER, SQUARES, SCALE, STORE, PUT = -1, 0, 1, 2, 3, 4, 5, 6

GR = H + 1
SUM_ROWS = -(-(N + P) // P) * P

assert RING <= RAW < FIRST and sorted(ZEROS_ACT + ZEROS_DVE) == list(range(-(-(XN + 1) // XL)))
assert REST == 2 and TAIL < P and RING % 2 == 0 and NP < LAST <= P
assert N == 2 * (CHUNKS * NP + LAST) and N == 4 * (XN * P + XLAST) and ENDS == 3


def gnn_kernel(nc, x, xT, srcT, dst, dstT, edgeT, mW1, mb1, mW2T, mb2, uW1, ub1, uW2, ub2, out):
    table_src = nc.dram_tensor("table_src", (N, H), F32, kind="Internal").ap()
    table_dst = nc.dram_tensor("table_dst", (N, H), F32, kind="Internal").ap()
    sums_d = nc.dram_tensor("sums_d", (SUM_ROWS, GR), F32, kind="Internal").ap()

    with ExitStack() as ctx:
        def sb(name, shape, dt=F32):
            return ctx.enter_context(nc.sbuf_tensor(name, shape, dt))

        def pb(name, shape):
            return ctx.enter_context(nc.psum_tensor(name, shape, F32))

        def sem(name):
            return ctx.enter_context(nc.semaphore(name))

        agg = sb("agg", [P, N])
        xdeg = sb("xdeg", [P, N])
        dst_rel = sb("dst_rel", [P, NG * TILES])
        start_b = sb("start_b", [P, NG])
        start_i = sb("start_i", [1, NG], I32)
        idx0 = sb("idx0", [P, FIRST * TILES], I32)
        idx = sb("idx", [P, RING, TILES], I32)
        raw_x = sb("raw_x", [P, RAW - RING, TILES, D])
        raw_t = sb("raw_t", [D, 2, GE])
        gath = sb("gath", [P, RING, GE])
        onehot = sb("onehot", [P, RING, TILES * WIN])
        lhs = sb("lhs", [P, RING, GE])
        rhs = sb("rhs", [P, RING, H])
        xwin = sb("xwin", [D + 1, RING, WIN])
        hid = sb("hid", [P, RING, GE])
        deg = sb("deg", [P, RING])
        ident = sb("ident", [P, P])
        iota = sb("iota", [P, WIN])
        ones = sb("ones", [P, P])
        w_src = sb("w_src", [P, H])
        w_dst = sb("w_dst", [D + 1, H])
        mw2t = sb("mw2t", [D, H])
        mb2c = sb("mb2c", [D, D + 1])
        uw1b = sb("uw1b", [D, H])
        w_agg = sb("w_agg", [H, H])
        w_x = sb("w_x", [D + 1, H])
        ub1c = sb("ub1c", [H, 1])
        uw2 = sb("uw2", [H, D])
        ub2r = sb("ub2r", [1, D])
        eps = sb("eps", [P, 1])
        upd = sb("upd", [H, ENDS, 2 * LAST])
        xrow = sb("xrow", [LAST, ENDS, 2, D])
        y = sb("y", [LAST, ENDS, 2, D])
        yc = sb("yc", [LAST, ENDS, 2, D])
        sq = sb("sq", [LAST, ENDS, 2, D])
        yout = sb("yout", [LAST, ENDS, 2, D])
        stat = sb("stat", [LAST, ENDS, 4, 2])
        low = sb("low", [ITERS, RING])
        high = sb("high", [ITERS, RING])
        late = sb("late", [ITERS, RING])
        bad = sb("bad", [ITERS, 1])
        bound = sb("bound", [ITERS, 1])
        dst_i = dst_rel[:, :].bitcast(I32)
        dst_x = sb("dst_x", [1, RE], I32)
        low_x = sb("low_x", [1, REST])
        high_x = sb("high_x", [1, REST])
        late_x = sb("late_x", [1, REST])
        bad_x = sb("bad_x", [1, 1])
        fits = sb("fits", [1, 1], I32)

        dst_s = lhs[0:ITERS, :, :].bitcast(I32)
        spread = onehot[0:ITERS, :, :].rearrange("p r n -> p (r n)")[:, 0:ITERS * RING].rearrange("p (i r) -> p i r", r=RING)
        rows = (gath, hid)
        g_e = lhs[WIN:P, 0, 0:P]
        g_w = rhs[WIN:P, 0, :]
        g_src = gath[:, 0, 0:H]
        g_dst = gath[:, 1, 0:H]
        g_old = gath[:, 2, 0:GR]
        g_new = gath[:, 3, 0:GR]
        g_h = hid[:, 0, 0:GR]
        g_same = lhs[:, 1, 0:P]
        g_less = lhs[:, 2, 0:P]
        g_tmp = lhs[:, 3, 0:P]
        g_col_b = lhs[:, 4, 0:P]
        g_spare, g_dcol, g_again, g_to = (deg[:, i:i + 1] for i in range(4))
        mb1b = onehot[:, 0, 0:H]
        g_isrc, g_idst, g_iout = (idx0[:, i:i + 1] for i in range(3))

        ps_turn = [pb(f"ps_turn{i}", [P, GE]) for i in range(2)]
        ps_pre = [pb(f"ps_pre{i}", [P, GE]) for i in range(2)]
        ps_sum = [pb(f"ps_sum{i}", [P, GE]) for i in range(2)]
        ps_node = pb("ps_node", [P, GE])
        ps_iota = pb("ps_iota", [P, GE])
        ps_ends = [ps_node, ps_turn[0], ps_pre[0]]

        weights_in = sem("weights_in")
        mb1_in = sem("mb1_in")
        node_w_in = sem("node_w_in")
        edge_w_in = sem("edge_w_in")
        w_dst_in = sem("w_dst_in")
        dst_in = [sem(f"dst_in{i}") for i in range(2)]
        stats_in = sem("stats_in")
        x_in = [sem(f"x_in{i}") for i in range(-(-(XN + 1) // XL))]
        memsets = sem("memsets")
        dst_made = sem("dst_made")
        consts = sem("consts")
        chain = sem("chain")
        rows_made = sem("rows_made")
        rows_out = [sem(f"rows_out{i}") for i in range(2)]
        rows_stored = [[sem(f"rows_stored{p}_{i}") for i in range(RING)] for p in range(2)]
        node_w = sem("node_w")
        node_w_out = sem("node_w_out")
        starts_made = sem("starts_made")
        bad_made = sem("bad_made")
        bad_summed = sem("bad_summed")
        starts_ready = sem("starts_ready")
        fits_ready = sem("fits_ready")
        cleared = sem("cleared")
        xdeg_zero_act = sem("xdeg_zero_act")
        xdeg_zero_dve = sem("xdeg_zero_dve")
        idx0_in = sem("idx0_in")
        idx_in = [sem(f"idx_in{i}") for i in range(RING)]
        raw_got = [sem(f"raw_got{i}") for i in range(RING)]
        raw_turned = sem("raw_turned")
        raw_copied = sem("raw_copied")
        edge_in = [sem(f"edge_in{i}") for i in range(RING)]
        win_in = [sem(f"win_in{i}") for i in range(RING)]
        win_made = sem("win_made")
        rhs_made = sem("rhs_made")
        gathered = [sem(f"gathered{i}") for i in range(RING)]
        onehot_made = sem("onehot_made")
        turned = sem("turned")
        lhs_made = sem("lhs_made")
        pre_made = sem("pre_made")
        hsum_made = sem("hsum_made")
        hid_made = sem("hid_made")
        summed = sem("summed")
        added = sem("added")
        xrow_in = [sem(f"xrow_in{i}") for i in range(ENDS)]
        upd_pre = sem("upd_pre")
        upd_made = sem("upd_made")
        y_pre = sem("y_pre")
        y_made = sem("y_made")
        var_made = sem("var_made")
        dev_made = sem("dev_made")
        yout_made = sem("yout_made")
        out_stored = [sem(f"out_stored{i}") for i in range(ENDS)]
        y_sum = sem("y_sum")
        yc_made = sem("yc_made")
        inv_made = sem("inv_made")
        passed = sem("passed")
        g_consts = sem("g_consts")
        g_step = sem("g_step")
        g_isrc_in = sem("g_isrc_in")
        g_idst_in = sem("g_idst_in")
        g_e_in = sem("g_e_in")
        g_zero = sem("g_zero")
        g_cleared = sem("g_cleared")
        g_src_got = sem("g_src_got")
        g_dst_got = sem("g_dst_got")
        g_old_got = sem("g_old_got")
        g_col = sem("g_col")
        g_mm = sem("g_mm")
        g_ready = sem("g_ready")
        g_comb = sem("g_comb")
        g_done = sem("g_done")
        g_put = sem("g_put")
        g_back = sem("g_back")
        g_turn = sem("g_turn")
        g_copied = sem("g_copied")

        block = ctx.enter_context(nc.Block())

        def after(eng, s, value):
            if not isinstance(value, int) or value > 0:
                eng.wait_ge(s, value)

        def let(eng):
            eng.sem_inc(passed, 1)

        def cols(start, count):
            return slice(start, start + count) if isinstance(start, int) else bass.ds(start, count)

        def group(it, k, back=0):
            it, k = it + (k - back) // RING, (k - back) % RING
            s = it * RING + k
            return None if isinstance(s, int) and not 0 <= s < NG else (s, it, k)

        def shape(s):
            return (1, TAIL) if isinstance(s, int) and s == NG - 1 else (TILES, P)

        def groups(eng, step, node, peeled=2):
            for it in range(peeled):
                for k in range(RING):
                    step(it, k)
            with eng.Fori(peeled, LAG) as it:
                for k in range(RING):
                    step(it, k)
            with eng.Fori(LAG, ITERS) as it:
                for k in range(RING):
                    step(it, k)
                    node(it - LAG, k, NP)

            def end(i, stage):
                c = ITERS - LAG + i
                node(c, stage, NP if c < CHUNKS else LAST, i)

            for i in range(ENDS):
                end(i, AHEAD)
            end(0, UPD)
            step(ITERS, 0)
            end(0, Y)
            step(ITERS, 1)
            step(ITERS, 2)
            step(ITERS, 3)
            end(0, CENTER)
            end(1, UPD)
            step(ITERS, 4)
            end(0, SQUARES)
            end(1, Y)
            end(0, SCALE)
            end(2, UPD)
            end(0, PUT)
            end(1, CENTER)
            end(2, Y)
            end(1, SQUARES)
            end(1, SCALE)
            end(1, PUT)
            end(2, CENTER)
            end(2, SQUARES)
            end(2, SCALE)
            end(2, PUT)

        def is_raw(s):
            return isinstance(s, int) and s < RAW

        def raw(s, j):
            return hid[:, s, j * H:j * H + D] if s < RING else raw_x[:, s - RING, j, :]

        def raw_sem(s):
            return raw_got[s] if s < RING else gathered[s - RING]

        def got(it, t):
            return (it - 1) * (16 * TILES) + 16 * t

        def begun(s):
            return isinstance(s, int) and s in EARLY.values()

        def src_by_tile(s, j, m, k):
            ap = idx0[0:m, s * TILES + j:s * TILES + j + 1] if isinstance(s, int) and s < FIRST else idx[0:m, k, j:j + 1]
            return bass.IndirectOffsetOnAxis(ap=ap, axis=0)

        HALVES = (slice(0, DFIRST * TILES), slice(DFIRST * TILES, NG * TILES))

        def free(c, slot):
            return c - slot if isinstance(c, int) else c

        def all_nodes(eng, node):
            for k in range(UPD, STORE + 1):
                node(0, k, NP)
            with eng.Fori(1, CHUNKS) as c:
                for k in range(UPD, STORE + 1):
                    node(c, k, NP)
            for k in range(UPD, STORE + 1):
                node(CHUNKS, k, LAST)

        def tiles(eng, tile):
            tile(0, P)
            with eng.Fori(1, ET - 1) as t:
                tile(t, P)
            tile(ET - 1, E - (ET - 1) * P)

        def blocks(eng, part):
            part(0, P)
            with eng.Fori(1, N // P) as b:
                part(b, P)
            part(N // P, N % P)

        def stored(eng, phase):
            for k in range(RING):
                eng.wait_ge(rows_stored[phase][k], 16 * sum(q % RING == k for q, _ in TABLE))

        def store_rows(eng, phase, q, m):
            eng.wait_ge(rows_out[phase], q + 1)
            to = (table_src, table_dst)[phase][q * XC:q * XC + 4 * m, :]
            eng.dma_start(to.rearrange("(p j) h -> p (j h)", j=4),
                          rows[phase][0:m, q % RING, :]).then_inc(rows_stored[phase][q % RING], 16)

        @block.sync
        def _(sp):
            def load_idx(s, it, k):
                sp.wait_ge(gathered[k], got(it - 1, TILES))
                sp.dma_start(idx[:, k, :], srcT[:, cols(s * TILES, TILES)]).then_inc(idx_in[k], 16)

            def load_x(i):
                at = slice(i * XL * XC, min((i + 1) * XL * XC, N))
                sp.dma_start(xdeg[0:D, at], xT[:, at]).then_inc(x_in[i], 16)

            def load_dst(half):
                at = HALVES[half]
                sp.dma_start(dst_i[:, at], dstT[:, at]).then_inc(dst_in[half], 16)

            def load_group(s, it, k):
                t, m = shape(s)
                after(sp, pre_made, s - RING + 1)
                sp.dma_start(lhs[WIN:P, k, 0:t * m], edgeT[:, cols(s * GE, t * m)]).then_inc(edge_in[k], 16)
                start = sp.value_load(start_i[0:1, cols(s, 1)], min_val=0, max_val=WMAX)
                sp.dma_start(xwin[0:D, k, :], xT[:, bass.ds(start, WIN)]).then_inc(win_in[k], 16)

            sp.dma_start(idx0[:, :], srcT[:, 0:FIRST * TILES]).then_inc(idx0_in, 16)
            load_x(0)
            whole = ITERS // 16 * 16
            by_iter = dst[0:ITERS * RING * GE].rearrange("(p r n) -> p r n", p=ITERS, r=RING)
            sp.dma_start(dst_s[0:whole, :, :], by_iter[0:whole, :, :]).then_inc(stats_in, 16)
            sp.dma_start(dst_s[whole:ITERS, :, :], by_iter[whole:ITERS, :, :]).then_inc(stats_in, 16)
            sp.dma_start(dst_x[:, :], dst[E - RE:E].rearrange("(a n) -> a n", a=1)).then_inc(stats_in, 16)
            load_x(1)
            load_x(2)
            edge_w = mW1[2 * D:, :].rearrange("p (a h) -> p a h", a=1).broadcast_to([DE, RING, H])
            small = [(rhs[WIN:P, :, :], edge_w, edge_w_in)] + [(to, a, node_w_in) for to, a in (
                (mw2t[:, :], mW2T), (mb2c[:, D:D + 1], mb2), (uw1b[:, :], uW1[D:, :]), (w_x[0:D, :], uW1[0:D, :]),
                (ub1c[:, :], ub1), (uw2[:, :], uW2), (ub2r[:, :], ub2))]
            for q, m in TABLE:
                store_rows(sp, 0, q, m)
                if q % XL == 1 and q // XL + 3 < len(x_in):
                    load_x(q // XL + 3)
                if q == Q_DST:
                    load_dst(0)
                    sp.dma_start(w_dst[0:D, :], mW1[D:2 * D, :]).then_inc(w_dst_in, 16)
                    sp.dma_start(w_dst[D:D + 1, :], mb1).then_inc(w_dst_in, 16)
                if q == Q_LOADS:
                    sp.wait_ge(starts_ready, 1)
                    for g in EARLY.values():
                        load_group(g, 0, g)
                if q < len(small):
                    sp.dma_start(small[q][0], small[q][1]).then_inc(small[q][2], 16)
            sp.wait_ge(fits_ready, 1)
            fit = sp.value_load(fits[0:1, 0:1], min_val=0, max_val=1)

            def step(it, k):
                if not group(it, k):
                    return
                s, _, _ = group(it, k)
                if isinstance(s, int) and s == 4:
                    load_dst(1)
                later = group(it, k, -LOOK)
                if later and not (isinstance(later[0], int) and later[0] < FIRST):
                    load_idx(*later)
                if not begun(s):
                    load_group(s, it, k)

            def node(c, k, m, i=0):
                if k in (STORE, AHEAD):
                    after(sp, y_made, free(c, i))
                    sp.dma_start(xrow[0:m, i, :, :], x[cols(c * NC, 2 * m), :].rearrange("(p j) f -> p j f", j=2)).then_inc(xrow_in[i], 16)

            with sp.If(fit == 1):
                groups(sp, step, node)
                for i in range(ENDS):
                    sp.wait_ge(out_stored[i], 16 if i else 16 * (ITERS - LAG + 1))
            with sp.Else():
                for g in EARLY.values():
                    sp.wait_ge(edge_in[g], 16)
                    sp.wait_ge(win_in[g], 16)
                sp.wait_ge(turned, len(EARLY))
                sp.dma_start(mb1b, mb1.broadcast_to([P, H])).then_inc(mb1_in, 16)
                sp.wait_ge(g_zero, 1)
                sp.dma_start(sums_d.rearrange("(r p) g -> p r g", p=P),
                             g_new.rearrange("p (a g) -> p a g", a=1).broadcast_to([P, SUM_ROWS // P, GR])).then_inc(g_cleared, 16)

                def load(t, m):
                    if isinstance(t, int) and t == 0:
                        sp.wait_ge(idx0_in, 16)
                        for k in range(RAW):
                            sp.wait_ge(raw_sem(k), 16 * TILES)
                    after(sp, g_put, t * 16)
                    let(sp)
                    sp.dma_start(g_isrc[0:m, :], srcT[0:m, cols(t, 1)], allow_slow_non_contiguous=True).then_inc(g_isrc_in, 16)
                    sp.dma_start(g_idst[0:m, :], dstT[0:m, cols(t, 1)], allow_slow_non_contiguous=True).then_inc(g_idst_in, 16)
                    sp.dma_start(g_e[:, 0:m], edgeT[:, cols(t * P, m)]).then_inc(g_e_in, 16)

                tiles(sp, load)
                sp.wait_ge(g_put, 16 * ET)

                def back(b, m):
                    after(sp, g_turn, b)
                    sp.dma_start(g_old[0:m, :], sums_d[cols(b * P, m), :]).then_inc(g_back, 16)

                blocks(sp, back)
                all_nodes(sp, node)
                sp.wait_ge(out_stored[0], 16 * (CHUNKS + 1))

        @block.gpsimd
        def _(pool):
            def then(n, ins):
                ins.then_inc(consts, 1)
                pool.wait_ge(consts, n)

            then(1, nc.gpsimd.memset(ones[:, :], 1.0))
            then(2, nc.gpsimd.memset(ident[:, :], 1.0))
            then(3, nc.gpsimd.affine_select(out=ident[:, :], in_=ident[:, :], compare_op=ALU.is_equal, fill=0.0, base=0,
                                            pattern=[[-1, P]], channel_multiplier=1))
            then(4, nc.gpsimd.iota(iota[:, :], [[1, WIN]], base=0, channel_multiplier=0,
                                   allow_small_or_imprecise_dtypes=True))
            then(5, nc.gpsimd.iota(bound[:, :], [[0, 1]], base=NC * (2 - LAG), channel_multiplier=NC,
                                   allow_small_or_imprecise_dtypes=True))
            then(6, nc.gpsimd.memset(mb2c[:, 0:D], 0.0))
            then(7, nc.gpsimd.memset(eps[:, :], EPS))
            then(8, nc.gpsimd.memset(xwin[D:D + 1, :, :], 1.0))
            pool.wait_ge(idx0_in, 16)
            for g in range(RAW):
                for j in range(TILES):
                    pool.indirect_dma_start(raw(g, j), None, x,
                                            src_by_tile(g, j, P, g % RING)).then_inc(raw_sem(g), 16)
            pool.wait_ge(fits_ready, 1)
            fit = pool.value_load(fits[0:1, 0:1], min_val=0, max_val=1)
            stored(pool, 0)

            def step(it, k):
                if not group(it, k) or is_raw(group(it, k)[0]):
                    return
                s, _, _ = group(it, k)
                t, m = shape(s)
                if not (isinstance(s, int) and s < FIRST):
                    pool.wait_ge(idx_in[k], it * 16 - 16)
                if isinstance(s, int) and is_raw(s - RING):
                    after(pool, gathered[k], got(it, 0))
                else:
                    after(pool, hsum_made, s - RING + 1)
                let(pool)
                for j in range(t):
                    pool.indirect_dma_start(gath[0:m, k, j * H:(j + 1) * H], None, table_src,
                                            src_by_tile(s, j, m, k)).then_inc(gathered[k], 16)

            with pool.If(fit == 1):
                groups(pool, step, lambda *chunk: None, peeled=3)
            with pool.Else():
                stored(pool, 1)
                pool.wait_ge(lhs_made, len(EARLY))
                nc.gpsimd.memset(g_less, 1.0).then_inc(memsets, 1)
                pool.wait_ge(memsets, 1)
                nc.gpsimd.affine_select(out=g_less, in_=g_less, compare_op=ALU.is_gt, fill=0.0, base=0,
                                        pattern=[[-1, P]], channel_multiplier=1).then_inc(g_consts, 1)
                nc.gpsimd.iota(g_spare, [[0, 1]], base=N, channel_multiplier=1,
                               allow_small_or_imprecise_dtypes=True).then_inc(g_consts, 1)
                pool.wait_ge(g_cleared, 16)

                def tile(t, m):
                    pool.wait_ge(g_isrc_in, t * 16 + 16)
                    pool.wait_ge(g_idst_in, t * 16 + 16)
                    after(pool, g_put, t * 16)
                    let(pool)
                    for got, table, ix, done in ((g_src, table_src, g_isrc, g_src_got), (g_dst, table_dst, g_idst, g_dst_got),
                                                 (g_old, sums_d, g_idst, g_old_got)):
                        pool.indirect_dma_start(got[0:m, :], None, table,
                                                bass.IndirectOffsetOnAxis(ap=ix[0:m, :], axis=0)).then_inc(done, 16)
                    pool.wait_ge(g_done, t + 1)
                    let(pool)
                    pool.indirect_dma_start(sums_d, bass.IndirectOffsetOnAxis(ap=g_iout[0:m, :], axis=0),
                                            g_new[0:m, :], None).then_inc(g_put, 16)

                tiles(pool, tile)

        @block.tensor
        def _(pe):
            pe.wait_ge(weights_in, 16)

            def window(s, it, k):
                pe.wait_ge(win_in[k], it * 16 + 16)
                after(pe, added, 2 * (s - 3))
                nc.tensor.matmul(ps_sum[k % 2][0:WIN, 2 * P:3 * P], xwin[:, k, :], w_dst[:, :],
                                 start=True, stop=True).then_inc(win_made, 1)

            def turn(s, it, k):
                t, m = shape(s)
                pe.wait_ge(onehot_made, s + 1)
                after(pe, lhs_made, s - 1)
                for j in range(t):
                    mm = nc.tensor.transpose(ps_turn[k % 2][0:WIN, j * P:j * P + m],
                                             onehot[0:m, k, j * WIN:(j + 1) * WIN], ident[0:m, 0:m])
                mm.then_inc(turned, 1)

            def turn_raw(s, it, k):
                pe.wait_ge(raw_sem(s), 16 * TILES)
                pe.wait_ge(raw_copied, s) if s else pe.wait_ge(node_w_out, 2)
                for j in range(TILES):
                    mm = nc.tensor.transpose(ps_node[0:D, j * P:(j + 1) * P], raw(s, j), ident[:, :])
                mm.then_inc(raw_turned, 1)

            zeroed = {i: (xdeg_zero_act, n + 1) for n, i in enumerate(ZEROS_ACT)}
            zeroed |= {i: (xdeg_zero_dve, n + 2) for n, i in enumerate(ZEROS_DVE)}

            def make_rows(phase):
                kk, w = ((P, w_src), (D, w_dst))[phase]
                for q, m in TABLE:
                    pe.wait_ge(x_in[q // XL], 16)
                    pe.wait_ge(*zeroed[q // XL])
                    after(pe, rows_out[phase], q - 1)
                    for j in range(4):
                        mm = nc.tensor.matmul(ps_pre[q % 2][0:m, j * H:(j + 1) * H], xdeg[0:kk, q * XC + j:q * XC + 4 * m:4],
                                              w[0:kk, :], start=True, stop=True)
                    mm.then_inc(rows_made, 1)
                    if phase == 0 and q == Q_FITS:
                        pe.wait_ge(bad_made, 2)
                        pe.wait_ge(starts_made, 1)
                        nc.tensor.matmul(ps_sum[0][0:1, NG:NG + 1], bad[:, :], ones[0:ITERS, 0:1], start=True, stop=False)
                        nc.tensor.matmul(ps_sum[0][0:1, NG:NG + 1], bad_x[:, :], ones[0:1, 0:1], start=False, stop=True)
                        nc.tensor.matmul(ps_sum[0][:, 0:ITERS * RING], ones[0:ITERS, :], spread[:, :, :].rearrange("p i k -> p (i k)"),
                                         start=True, stop=True)
                        nc.tensor.matmul(ps_sum[0][:, ITERS * RING:NG], ones[0:1, :], low_x[:, :],
                                         start=True, stop=True).then_inc(bad_summed, 1)
                    if phase == 0 and q in EARLY:
                        g = EARLY[q]
                        if g == 0:
                            pe.wait_ge(starts_ready, 1)
                            pe.wait_ge(w_dst_in, 32)
                        window(g, 0, g)
                        turn(g, 0, g)
                        turn_raw(g, 0, g)
                    if phase == 0 and q == Q_WEIGHTS:
                        pe.wait_ge(node_w_in, 16 * 7)
                        nc.tensor.matmul(ps_node[:, 0:H], mw2t[:, :], uw1b[:, :], start=True, stop=True)
                        nc.tensor.matmul(ps_node[0:D + 1, H:2 * H], mb2c[:, :], uw1b[:, :], start=True, stop=True).then_inc(node_w, 1)

            make_rows(0)
            pe.wait_ge(fits_ready, 1)
            pe.wait_ge(rows_out[0], len(TABLE))
            pe.wait_ge(edge_w_in, 16)
            fit = pe.value_load(fits[0:1, 0:1], min_val=0, max_val=1)

            def pre(s, it, k):
                t, m = shape(s)
                pe.wait_ge(lhs_made, s + 1)
                pe.wait_ge(edge_in[k], it * 16 + 16)
                pe.wait_ge(rhs_made, s + 1)
                if is_raw(s):
                    pe.wait_ge(raw_copied, s + 1)
                after(pe, hsum_made, s - 1)
                for j in range(t):
                    to = ps_pre[k % 2][0:m, j * H:(j + 1) * H]
                    mm = nc.tensor.matmul(to, lhs[:, k, j * P:j * P + m], rhs[:, k, :], start=True, stop=not is_raw(s))
                    if is_raw(s):
                        mm = nc.tensor.matmul(to, raw_t[:, k % 2, j * P:(j + 1) * P], w_src[0:D, :], start=False, stop=True)
                mm.then_inc(pre_made, 1)

            def summing(s, it, k):
                t, m = shape(s)
                pe.wait_ge(hid_made, s + 1)
                after(pe, added, 2 * (s - 1))
                pe.wait_ge(rhs_made, s + 3 if not isinstance(s, int) else min(s + 3, NG))
                for j in range(t):
                    nc.tensor.matmul(ps_sum[k % 2][:, 0:WIN], hid[0:m, k, j * H:(j + 1) * H],
                                     onehot[0:m, k, j * WIN:(j + 1) * WIN], start=(j == 0), stop=(j == t - 1))
                nc.tensor.matmul(ps_sum[k % 2][:, P:P + WIN], deg[0:WIN, k:k + 1].broadcast_to([WIN, P]), ident[0:WIN, 0:WIN],
                                 start=True, stop=True).then_inc(summed, 1)

            def step(it, k):
                for back, stage in ((0, turn), (0, turn_raw), (1, pre), (2, summing), (-1, window)):
                    at = group(it, k, back)
                    if at and not (stage != pre and stage != summing and begun(at[0])) and (stage != turn_raw or is_raw(at[0])):
                        stage(*at)

            def node(c, k, m, i=0, general=False):
                bank = ps_ends[i]
                if k == UPD:
                    if general:
                        pe.wait_ge(g_copied, 2 * (N // P + 1))
                    else:
                        last = (c + (LAG - 1)) * RING
                        pe.wait_ge(added, 2 * min(last, NG) if isinstance(c, int) else 2 * last)
                    after(pe, y_made, free(c, i))
                    if isinstance(c, int) or not general:
                        pe.wait_ge(node_w_out, 2)
                    at = cols(c * NC, 2 * m)
                    nc.tensor.matmul(bank[:, 0:2 * m], w_agg[:, :], agg[:, at], start=True, stop=False)
                    nc.tensor.matmul(bank[:, 0:2 * m], w_x[:, :], xdeg[0:D + 1, at], start=False, stop=True).then_inc(upd_pre, 1)
                if k == Y:
                    pe.wait_ge(upd_made, c + 1)
                    for j in range(2):
                        to = bank[0:m, 2 * P + j * D:2 * P + (j + 1) * D]
                        nc.tensor.matmul(to, upd[:, i, j:2 * m:2], uw2[:, :], start=True, stop=False)
                        mm = nc.tensor.matmul(to, ones[0:1, 0:m], ub2r[:, 0:D], start=False, stop=True)
                    mm.then_inc(y_pre, 1)

            with pe.If(fit == 1):
                groups(pe, step, node)
            with pe.Else():
                pe.wait_ge(lhs_made, len(EARLY))
                pe.wait_ge(rhs_made, len(EARLY))
                pe.wait_ge(raw_copied, len(EARLY))
                make_rows(1)

                def tile(t, m):
                    pe.wait_ge(g_e_in, t * 16 + 16)
                    pe.wait_ge(g_col, t + 1)
                    nc.tensor.matmul(ps_pre[0][0:m, 0:H], g_e[:, 0:m], g_w, start=True, stop=True)
                    nc.tensor.transpose(ps_turn[0][0:m, 0:m], g_col_b[0:m, 0:m], ident[0:m, 0:m]).then_inc(g_mm, 1)
                    pe.wait_ge(g_ready, t + 1)
                    nc.tensor.matmul(ps_sum[0][0:m, 0:GR], g_same[0:m, 0:m], g_h[0:m, :], start=True, stop=True).then_inc(g_comb, 1)

                tiles(pe, tile)

                def part(b, m):
                    pe.wait_ge(g_back, b * 16 + 16)
                    after(pe, g_copied, 2 * b)
                    nc.tensor.transpose(ps_turn[0][:, 0:m], g_old[0:m, 0:H], ident[0:m, 0:m])
                    nc.tensor.transpose(ps_turn[1][0:D + 1, 0:m], g_old[0:m, GR - D - 1:GR], ident[0:m, 0:m]).then_inc(g_turn, 1)

                blocks(pe, part)
                all_nodes(pe, lambda c, k, m: node(c, k, m, 0, True))

        @block.scalar
        def _(act):
            act.dma_start(w_src[0:D, :], mW1[0:D, :]).then_inc(weights_in, 16)
            act.wait_ge(consts, 1)

            def zeros(i):
                to = xdeg[D:P, i * XL * XC:min((i + 1) * XL * XC, N)]
                nc.scalar.activation(to, ones[D:P, 0:1].broadcast_to([P - D, to.shape[1]]), ACT.Copy, scale=0.0).then_inc(xdeg_zero_act, 1)

            for i in ZEROS_ACT:
                zeros(i)

            def copy_turned(s, it, k):
                t, m = shape(s)
                act.wait_ge(turned, s + 1)
                after(act, summed, s - RING + 1)
                nc.scalar.activation(lhs[0:WIN, k, 0:t * m], ps_turn[k % 2][0:WIN, 0:t * m], ACT.Copy,
                                     accum_out=deg[0:WIN, k:k + 1]).then_inc(lhs_made, 1)

            def copy_raw(s, it, k):
                act.wait_ge(raw_turned, s + 1)
                after(act, pre_made, s - 1)
                nc.scalar.copy(raw_t[:, k % 2, :], ps_node[0:D, :]).then_inc(raw_copied, 1)

            def copy_window(s, it, k):
                act.wait_ge(win_made, s + 1)
                after(act, pre_made, s - RING + 1)
                nc.scalar.copy(rhs[0:WIN, k, :], ps_sum[k % 2][0:WIN, 2 * P:3 * P]).then_inc(rhs_made, 1)

            for q, m in TABLE:
                act.wait_ge(rows_made, q + 1)
                after(act, rows_stored[0][q % RING], q // RING * 16)
                nc.scalar.copy(rows[0][0:m, q % RING, :], ps_pre[q % 2][0:m, :]).then_inc(rows_out[0], 1)
                if q in EARLY:
                    g = EARLY[q]
                    copy_window(g, 0, g)
                    copy_turned(g, 0, g)
                    copy_raw(g, 0, g)
                if q == Q_WEIGHTS:
                    act.wait_ge(node_w, 1)
                    nc.scalar.copy(w_agg[:, :], ps_node[:, 0:H]).then_inc(node_w_out, 1)
                    nc.scalar.copy(w_x[D:D + 1, :], ps_node[D:D + 1, H:2 * H]).then_inc(node_w_out, 1)
            act.wait_ge(fits_ready, 1)
            fit = act.value_load(fits[0:1, 0:1], min_val=0, max_val=1)

            def relu(s, it, k):
                t, m = shape(s)
                if is_raw(s):
                    after(act, summed, s - RING + 1)
                    act.wait_ge(pre_made, s + 1)
                    nc.scalar.activation(hid[:, k, :], ps_pre[k % 2][:, :], ACT.Relu).then_inc(hid_made, 1)
                    act.wait_ge(hid_made, s + 1)
                    act.sem_inc(hsum_made, 1)
                    return
                act.wait_ge(hsum_made, s + 1)
                h = hid[0:m, k, 0:t * H]
                nc.scalar.activation(h, h, ACT.Relu).then_inc(hid_made, 1)

            def step(it, k):
                for back, stage in ((0, copy_turned), (0, copy_raw), (1, relu), (-1, copy_window)):
                    at = group(it, k, back)
                    if at and not (stage != relu and begun(at[0])) and (stage != copy_raw or is_raw(at[0])):
                        stage(*at)

            def node(c, k, m, i=0):
                if k == UPD:
                    act.wait_ge(upd_pre, c + 1)
                    after(act, y_pre, free(c, i))
                    nc.scalar.activation(upd[:, i, 0:2 * m], ps_ends[i][:, 0:2 * m], ACT.Relu, bias=ub1c[:, 0:1]).then_inc(upd_made, 1)
                if k == SQUARES:
                    act.wait_ge(yc_made, c + 1)
                    after(act, yout_made, free(c, i))
                    for j in range(2):
                        nc.scalar.activation(sq[0:m, i, j, :], yc[0:m, i, j, :], ACT.Square,
                                             accum_out=stat[0:m, i, 2, j:j + 1]).then_inc(var_made, 1)
                    act.wait_ge(var_made, 2 * c + 2)
                    nc.scalar.activation(stat[0:m, i, 3, :], stat[0:m, i, 2, :], ACT.Sqrt, bias=eps[0:m, 0:1],
                                         scale=1.0 / D).then_inc(dev_made, 1)
                if k in (STORE, PUT):
                    act.wait_ge(yout_made, c + 1)
                    act.dma_start(out[cols(c * NC, 2 * m), :].rearrange("(p j) f -> p j f", j=2),
                                  yout[0:m, i, :, :]).then_inc(out_stored[i], 16)

            with act.If(fit == 1):
                groups(act, step, node)
            with act.Else():
                for q, m in TABLE:
                    store_rows(act, 1, q, m)

                def part(b, m):
                    act.wait_ge(g_turn, b + 1)
                    at = cols(b * P, m)
                    nc.scalar.copy(agg[:, at], ps_turn[0][:, 0:m]).then_inc(g_copied, 1)
                    nc.scalar.copy(xdeg[D:D + 1, at], ps_turn[1][D:D + 1, 0:m]).then_inc(g_copied, 1)

                act.wait_ge(cleared, 1)
                blocks(act, part)
                all_nodes(act, node)

        @block.vector
        def _(dve):
            steps = [0]

            def link(ins):
                steps[0] += 1
                ins.then_inc(chain, 1)
                dve.wait_ge(chain, steps[0])

            def zeros(i):
                nc.vector.memset(xdeg[D:P, i * XL * XC:min((i + 1) * XL * XC, N)], 0.0).then_inc(xdeg_zero_dve, 1)

            for i in ZEROS_DVE[0:2]:
                zeros(i)
                if i == 0:
                    nc.vector.memset(w_src[D:P, :], 0.0).then_inc(xdeg_zero_dve, 1)
            dve.wait_ge(consts, 8)
            dve.wait_ge(stats_in, 48)
            nc.vector.tensor_reduce(low[:, :], dst_s, AX_X, ALU.min)
            link(nc.vector.tensor_reduce(high[:, :], dst_s, AX_X, ALU.max))
            for g, (a, b) in enumerate(((0, GE), (GE, RE))):
                nc.vector.tensor_reduce(low_x[:, g:g + 1], dst_x[:, a:b], AX_X, ALU.min)
                link(nc.vector.tensor_reduce(high_x[:, g:g + 1], dst_x[:, a:b], AX_X, ALU.max))
            sets = ((low[:, :], high[:, :], late[:, :], bad[:, :], bound[:, 0:1]),
                    (low_x[:, :], high_x[:, :], late_x[:, :], bad_x[:, :], float(NC * (ITERS + 2 - LAG))))
            for lo, hi, la, ba, bd in sets:
                link(nc.vector.tensor_scalar(lo, lo, float(WMAX), None, ALU.min))
                link(nc.vector.tensor_tensor(hi, hi, lo, ALU.subtract))
                nc.vector.tensor_scalar(hi, hi, float(WIN - 1), 0.0, ALU.subtract, ALU.max)
                link(nc.vector.tensor_scalar(la, lo, bd, -1.0, ALU.subtract, ALU.mult))
                link(nc.vector.tensor_scalar(la, la, 0.0, None, ALU.max))
                link(nc.vector.tensor_tensor(hi, hi, la, ALU.add))
                nc.vector.tensor_reduce(ba, hi, AX_X, ALU.add).then_inc(bad_made, 1)
            low_by_row = low[:, :].rearrange("p (a r) -> p a r", a=1).broadcast_to([ITERS, ITERS, RING])
            diagonal = ident[0:ITERS, 0:ITERS].rearrange("p (i a) -> p i a", a=1).broadcast_to([ITERS, ITERS, RING])
            nc.vector.tensor_tensor(spread[:, :, :], low_by_row, diagonal, ALU.mult).then_inc(starts_made, 1)
            zeros(ZEROS_DVE[2])
            dve.wait_ge(bad_summed, 1)
            nc.vector.tensor_scalar(fits[:, :], ps_sum[0][0:1, NG:NG + 1], 0.0, None, ALU.is_equal).then_inc(fits_ready, 1)
            nc.vector.tensor_copy(start_i[:, :], ps_sum[0][0:1, 0:NG])
            link(nc.vector.tensor_copy(start_b[:, :], ps_sum[0][:, 0:NG]))

            def relative(half):
                at = HALVES[half]
                groups_of = slice(at.start // TILES, at.stop // TILES)
                dve.wait_ge(dst_in[half], 16)
                nc.vector.tensor_copy(dst_rel[:, at], dst_i[:, at]).then_inc(dst_made, 1)
                dve.wait_ge(dst_made, 2 * half + 1)
                by_group = dst_rel[:, at].rearrange("p (s t) -> p s t", t=TILES)
                count = groups_of.stop - groups_of.start
                starts = start_b[:, groups_of].rearrange("p (s a) -> p s a", a=1)
                nc.vector.tensor_tensor(by_group, by_group, starts.broadcast_to([P, count, TILES]), ALU.subtract).then_inc(dst_made, 1)
                dve.wait_ge(dst_made, 2 * half + 2)

            relative(0)
            link(nc.vector.tensor_copy(ps_iota[:, 0:WIN], iota[:, :]))
            dve.sem_inc(starts_ready, 1)

            def onehots(s, it, k):
                t, m = shape(s)
                after(dve, summed, s - RING + 1)
                to = onehot[0:m, k, 0:t * WIN].rearrange("p (t w) -> p t w", t=t)
                at = dst_rel[0:m, cols(s * TILES, t)].rearrange("p (t a) -> p t a", a=1)
                nums = ps_iota[0:m, 0:WIN].rearrange("p (a w) -> p a w", a=1)
                nc.vector.tensor_tensor(to, nums.broadcast_to([m, t, WIN]), at.broadcast_to([m, t, WIN]),
                                        ALU.is_equal).then_inc(onehot_made, 1)

            for g in EARLY.values():
                onehots(g, 0, g)
            for i in ZEROS_DVE[3:]:
                zeros(i)
            nc.vector.memset(agg[:, :], 0.0).then_inc(cleared, 1)

            dve.wait_ge(fits_ready, 1)
            fit = dve.value_load(fits[0:1, 0:1], min_val=0, max_val=1)

            def add_gathered(s, it, k):
                t, m = shape(s)
                if is_raw(s):
                    return
                if isinstance(s, int) and is_raw(s - 1):
                    dve.wait_ge(hsum_made, RAW)
                dve.wait_ge(pre_made, s + 1)
                dve.wait_ge(gathered[k], got(it, t))
                after(dve, summed, s - RING + 1)
                nc.vector.tensor_tensor(hid[0:m, k, 0:t * H], ps_pre[k % 2][0:m, 0:t * H], gath[0:m, k, 0:t * H],
                                        ALU.add).then_inc(hsum_made, 1)

            ends = {}

            def add_sums(s, it, k):
                dve.wait_ge(summed, s + 1)
                after(dve, added, 2 * s)
                if isinstance(s, int) and s in ends:
                    start = ends[s]
                else:
                    start = dve.value_load(start_i[0:1, cols(s, 1)], min_val=0, max_val=WMAX)
                at = bass.ds(start, WIN)
                nc.vector.tensor_tensor(agg[:, at], agg[:, at], ps_sum[k % 2][:, 0:WIN], ALU.add).then_inc(added, 1)
                nc.vector.tensor_tensor(xdeg[D:D + 1, at], xdeg[D:D + 1, at], ps_sum[k % 2][D:D + 1, P:P + WIN],
                                        ALU.add).then_inc(added, 1)

            def step(it, k):
                if isinstance(it, int) and (it, k) == (1, 0):
                    relative(1)
                if isinstance(it, int) and (it, k) == (ITERS, 0):
                    for g in range(NG - REST, NG):
                        ends[g] = dve.value_load(start_i[0:1, g:g + 1], min_val=0, max_val=WMAX)
                for back, stage in ((1, add_gathered), (-1, onehots), (3, add_sums)):
                    if group(it, k, back) and not (stage == onehots and begun(group(it, k, back)[0])):
                        stage(*group(it, k, back))

            def node(c, k, m, i=0):
                whole = [m, 2, D]
                if k == CENTER:
                    dve.wait_ge(y_pre, c + 1)
                    dve.wait_ge(xrow_in[i], 16 if i else c * 16 + 16)
                    after(dve, yout_made, free(c, i))
                    nc.vector.tensor_tensor(y[0:m, i, :, :], ps_ends[i][0:m, 2 * P:2 * P + 2 * D].rearrange("p (j f) -> p j f", j=2),
                                            xrow[0:m, i, :, :], ALU.add).then_inc(y_made, 1)
                    dve.wait_ge(y_made, c + 1)
                    nc.vector.tensor_reduce(stat[0:m, i, 1, :], y[0:m, i, :, :], AX_X, ALU.add).then_inc(y_sum, 1)
                    dve.wait_ge(y_sum, c + 1)
                    total = stat[0:m, i, 1, :].rearrange("p (j a) -> p j a", a=1)
                    nc.vector.scalar_tensor_tensor(out=yc[0:m, i, :, :], in0=total.broadcast_to(whole), scalar=-1.0 / D,
                                                   in1=y[0:m, i, :, :], op0=ALU.mult, op1=ALU.add).then_inc(yc_made, 1)
                if k == SCALE:
                    dve.wait_ge(dev_made, c + 1)
                    after(dve, out_stored[i], 0 if i else c * 16)
                    nc.vector.reciprocal(stat[0:m, i, 0, :], stat[0:m, i, 3, :]).then_inc(inv_made, 1)
                    dve.wait_ge(inv_made, c + 1)
                    inv = stat[0:m, i, 0, :].rearrange("p (j a) -> p j a", a=1)
                    nc.vector.tensor_tensor(yout[0:m, i, :, :], yc[0:m, i, :, :], inv.broadcast_to(whole), ALU.mult).then_inc(yout_made, 1)

            dve.wait_ge(cleared, 1)
            dve.wait_ge(node_w_in, 16 * 7)
            with dve.If(fit == 1):
                groups(dve, step, node)
            with dve.Else():
                dve.wait_ge(mb1_in, 16)
                for g in range(RAW):
                    dve.wait_ge(raw_sem(g), 16 * TILES)
                for q, m in TABLE:
                    dve.wait_ge(rows_made, len(TABLE) + q + 1)
                    after(dve, rows_stored[1][q % RING], q // RING * 16)
                    nc.vector.tensor_tensor(rows[1][0:m, q % RING, :].rearrange("p (j h) -> p j h", j=4),
                                            ps_pre[q % 2][0:m, :].rearrange("p (j h) -> p j h", j=4),
                                            mb1b[0:m, :].rearrange("p (a h) -> p a h", a=1).broadcast_to([m, 4, H]),
                                            ALU.add).then_inc(rows_out[1], 1)
                dve.wait_ge(lhs_made, len(EARLY))
                stored(dve, 1)
                nc.vector.memset(g_new, 0.0).then_inc(g_zero, 1)
                link(nc.vector.memset(g_h[:, H:GR], 1.0))
                dve.wait_ge(g_consts, 2)
                dve.wait_ge(g_cleared, 16)

                def tile(t, m):
                    def then(ins, n):
                        ins.then_inc(g_step, 1)
                        dve.wait_ge(g_step, t * 10 + n)

                    dve.wait_ge(g_idst_in, t * 16 + 16)
                    then(nc.vector.tensor_copy(g_dcol[0:m, :], g_idst[0:m, :]), 1)
                    nc.vector.tensor_copy(g_col_b[0:m, :], g_dcol[0:m, :].broadcast_to([m, P])).then_inc(g_col, 1)
                    dve.wait_ge(g_mm, t + 1)
                    then(nc.vector.tensor_scalar(g_same[0:m, 0:m], ps_turn[0][0:m, 0:m], g_dcol[0:m, :], None, ALU.is_equal), 2)
                    then(nc.vector.tensor_tensor(g_tmp[0:m, 0:m], g_same[0:m, 0:m], g_less[0:m, 0:m], ALU.mult), 3)
                    then(nc.vector.tensor_reduce(g_again[0:m, :], g_tmp[0:m, 0:m], AX_X, ALU.max), 4)
                    then(nc.vector.tensor_tensor(g_to[0:m, :], g_spare[0:m, :], g_dcol[0:m, :], ALU.subtract), 5)
                    then(nc.vector.tensor_tensor(g_to[0:m, :], g_to[0:m, :], g_again[0:m, :], ALU.mult), 6)
                    then(nc.vector.tensor_tensor(g_iout[0:m, :], g_to[0:m, :], g_dcol[0:m, :], ALU.add), 7)
                    for got in (g_src_got, g_dst_got, g_old_got):
                        dve.wait_ge(got, t * 16 + 16)
                    then(nc.vector.tensor_tensor(g_h[0:m, 0:H], g_src[0:m, :], g_dst[0:m, :], ALU.add), 8)
                    then(nc.vector.tensor_tensor(g_h[0:m, 0:H], g_h[0:m, 0:H], ps_pre[0][0:m, 0:H], ALU.add), 9)
                    then(nc.vector.tensor_scalar(g_h[0:m, 0:H], g_h[0:m, 0:H], 0.0, None, ALU.max), 10)
                    dve.sem_inc(g_ready, 1)
                    dve.wait_ge(g_comb, t + 1)
                    nc.vector.tensor_tensor(g_new[0:m, :], g_old[0:m, :], ps_sum[0][0:m, 0:GR], ALU.add).then_inc(g_done, 1)

                tiles(dve, tile)
                all_nodes(dve, node)


def kernel(**inputs):
    import numpy as _np
    import concourse.bacc as _bacc
    from concourse import mybir as _mybir
    from concourse.bass_utils import run_bass_kernel_spmd as _run

    given = {name: _np.asarray(a) for name, a in inputs.items()}

    def by_tile(a):
        return _np.pad(a, (0, NG * GE - E)).reshape(NG * TILES, P).T

    w = {name[len("L0_gnn_"):]: a for name, a in given.items() if name.startswith("L0_gnn_")}
    laid = [
        given["x"], given["x"].T, by_tile(given["src"]), given["dst"], by_tile(given["dst"]), given["edge_attr_32"].T,
        w["mW1"], w["mb1"].reshape(1, H), w["mW2"].T, w["mb2"].reshape(D, 1),
        w["uW1"], w["ub1"].reshape(H, 1), w["uW2"], w["ub2"].reshape(1, D),
    ]
    names = ["x", "xT", "srcT", "dst", "dstT", "edgeT", "mW1", "mb1", "mW2T", "mb2", "uW1", "ub1", "uW2", "ub2"]
    nc = _bacc.Bacc("TRN2", target_bir_lowering=False, num_devices=1)
    arrays, args = {}, []
    for name, a in zip(names, laid):
        a = _np.ascontiguousarray(a)
        arrays[f"in_{name}_dram"] = a
        args.append(nc.dram_tensor(f"in_{name}_dram", a.shape, _mybir.dt.from_np(a.dtype), kind="ExternalInput").ap())
    args.append(nc.dram_tensor("out_0_dram", (N, D), F32, kind="ExternalOutput").ap())
    gnn_kernel(nc, *args)
    r = _run(nc, [arrays], core_ids=[0])
    return r.results[0]["out_0_dram"]
```
